# Optimizing a Trainium2 kernel written in Bass

```python
import numpy as np
import jax
import jax.numpy as jnp

def _softmax(x, axis=-1):
    return jax.nn.softmax(x, axis=axis)

def _gelu(x):
    return jax.nn.gelu(x, approximate=True)

def _silu(x):
    return jax.nn.silu(x)

def _sigmoid(x):
    return jax.nn.sigmoid(x)

def _layernorm(x, axis=-1, eps=1e-05):
    m = jnp.mean(x, axis=axis, keepdims=True)
    v = jnp.var(x, axis=axis, keepdims=True)
    return (x - m) / jnp.sqrt(v + eps)

def _scatter_add(tgt, idx, src, axis=0):
    return tgt.at[idx].add(src)

def _segment_sum(src, seg, n):
    return jax.ops.segment_sum(src, seg, n)
kernel_name = 'mk_gps_d1_gnn_r16_39c862'

def setup_inputs(seed: int=0):
    np.random.seed(seed)
    _w = jnp.asarray

    def _rec_inputs():
        import jax
        import jax.numpy as jnp
        _gk = jax.random.key(seed)
        x = -0.0002117 + 1 * jax.random.normal(jax.random.fold_in(_gk, 1), (6250, 256), jnp.float32)
        src = jax.random.randint(jax.random.fold_in(_gk, 2), (100000,), 0, 6250, jnp.int32)
        dst = jnp.minimum((6250 * jax.random.uniform(jax.random.fold_in(_gk, 3), (100000,)) ** 2.0).astype(jnp.int32), 99999)
        _o = jnp.argsort(dst, stable=True)
        src = src[_o]
        dst = dst[_o]
        edge_weight = jax.random.uniform(jax.random.fold_in(_gk, 12), (100000,), jnp.float32, 0.0, 0.999998)
        return (x, src, dst, edge_weight)
    x, src, dst, edge_weight = _rec_inputs()

    def _L0_gnn_setup():
        import jax, jax.numpy as jnp
        import numpy as np
        N, D, E = (6250, 256, 312500)
        H = 2 * D
        EPS = 0.0
        key = jax.random.key(seed)
        k1, k2, k3, k4, k5, k6, k7 = jax.random.split(key, 7)
        x = jax.random.normal(k1, (N, D), dtype=jnp.float32)
        edge_index = jax.random.randint(k2, (2, E), 0, N, dtype=jnp.int64)
        edge_weight = jax.random.uniform(k3, (E,), dtype=jnp.float32)
        s1 = 1.0 / np.sqrt(D)
        s2 = 1.0 / np.sqrt(H)
        W1 = jax.random.uniform(k4, (D, H), dtype=jnp.float32, minval=-s1, maxval=s1)
        b1 = jax.random.uniform(k5, (H,), dtype=jnp.float32, minval=-s1, maxval=s1)
        W2 = jax.random.uniform(k6, (H, D), dtype=jnp.float32, minval=-s2, maxval=s2)
        b2 = jax.random.uniform(k7, (D,), dtype=jnp.float32, minval=-s2, maxval=s2)
        return {'x': x, 'edge_index': edge_index, 'edge_weight': edge_weight, 'W1': W1, 'b1': b1, 'W2': W2, 'b2': b2}
    _L0_gnn_all = _L0_gnn_setup()
    _L0_gnn_in = {k: v for k, v in _L0_gnn_all.items() if k in ('W1', 'b1', 'W2', 'b2')}
    del _L0_gnn_all

    def _L0_mix_setup():
        import jax, jax.numpy as jnp
        import numpy as np
        HEADS = 8
        EPS = 1e-05

        def _ln(t, w, b, headc):
            m = jnp.mean(t, axis=-1, keepdims=True)
            d = t - m
            std = jnp.sqrt(jnp.sum(d * d, axis=-1, keepdims=True) / (headc - 1))
            return w * (d / (std + EPS)) + b
        key = jax.random.key(seed)
        B, N, C = (32, 256, 256)
        headc = C // HEADS
        x = jax.random.normal(key, (B, N, C), dtype=jnp.float32)
        return {'x': x, 'kln_weight': jnp.ones((HEADS, 1, headc), dtype=jnp.float32), 'kln_bias': jnp.zeros((HEADS, 1, headc), dtype=jnp.float32), 'vln_weight': jnp.ones((HEADS, 1, headc), dtype=jnp.float32), 'vln_bias': jnp.zeros((HEADS, 1, headc), dtype=jnp.float32)}
    _L0_mix_all = _L0_mix_setup()
    _L0_mix_in = {k: v for k, v in _L0_mix_all.items() if k in ('kln_weight', 'kln_bias', 'vln_weight', 'vln_bias')}
    del _L0_mix_all

    def _L0_ffn_setup():
        import jax, jax.numpy as jnp
        import numpy as np
        B, S, H, F, E, K = (8, 256, 256, 512, 16, 2)
        EPS = 1e-05
        key = jax.random.key(seed)
        ks = jax.random.split(key, 9)
        sc = 0.02
        return {'x': jax.random.normal(ks[0], (B, S, H), dtype=jnp.float32), 'gate_w': jax.random.normal(ks[1], (H, E), dtype=jnp.float32) * sc, 'gate_b': jnp.zeros((E,), dtype=jnp.float32), 'w1': jax.random.normal(ks[2], (E, H, F), dtype=jnp.float32) * sc, 'b1': jnp.zeros((E, F), dtype=jnp.float32), 'w2': jax.random.normal(ks[3], (E, F, H), dtype=jnp.float32) * sc, 'b2': jnp.zeros((E, H), dtype=jnp.float32), 'gamma': jnp.ones((H,), dtype=jnp.float32), 'beta': jnp.zeros((H,), dtype=jnp.float32)}
    _L0_ffn_all = _L0_ffn_setup()
    _L0_ffn_in = {k: v for k, v in _L0_ffn_all.items() if k in ('gate_w', 'gate_b', 'w1', 'b1', 'w2', 'b2', 'gamma', 'beta')}
    del _L0_ffn_all
    return {'x': x, 'src': src, 'dst': dst, 'edge_weight': edge_weight, 'L0_gnn_W1': _L0_gnn_in['W1'], 'L0_gnn_b1': _L0_gnn_in['b1'], 'L0_gnn_W2': _L0_gnn_in['W2'], 'L0_gnn_b2': _L0_gnn_in['b2'], 'L0_mix_kln_weight': _L0_mix_in['kln_weight'], 'L0_mix_kln_bias': _L0_mix_in['kln_bias'], 'L0_mix_vln_weight': _L0_mix_in['vln_weight'], 'L0_mix_vln_bias': _L0_mix_in['vln_bias'], 'L0_ffn_gate_w': _L0_ffn_in['gate_w'], 'L0_ffn_gate_b': _L0_ffn_in['gate_b'], 'L0_ffn_w1': _L0_ffn_in['w1'], 'L0_ffn_b1': _L0_ffn_in['b1'], 'L0_ffn_w2': _L0_ffn_in['w2'], 'L0_ffn_b2': _L0_ffn_in['b2'], 'L0_ffn_gamma': _L0_ffn_in['gamma'], 'L0_ffn_beta': _L0_ffn_in['beta']}

def reference(x, src, dst, edge_weight, L0_gnn_W1, L0_gnn_b1, L0_gnn_W2, L0_gnn_b2, L0_mix_kln_weight, L0_mix_kln_bias, L0_mix_vln_weight, L0_mix_vln_bias, L0_ffn_gate_w, L0_ffn_gate_b, L0_ffn_w1, L0_ffn_b1, L0_ffn_w2, L0_ffn_b2, L0_ffn_gamma, L0_ffn_beta):
    import jax
    import jax.numpy as jnp

    def _L0_gnn_ref(x, edge_index, edge_weight, W1, b1, W2, b2):
        import jax, jax.numpy as jnp
        import numpy as np
        N, D, E = (6250, 256, 312500)
        H = 2 * D
        EPS = 0.0
        row, col = (edge_index[0], edge_index[1])
        messages = x[col] * edge_weight[:, None]
        agg = jax.ops.segment_sum(messages, row, num_segments=N)
        h = (1.0 + EPS) * x + agg
        h = jax.nn.relu(h @ W1 + b1)
        out = h @ W2 + b2
        return out

    def _L0_mix_ref(x, kln_weight, kln_bias, vln_weight, vln_bias):
        import jax, jax.numpy as jnp
        import numpy as np
        HEADS = 8
        EPS = 1e-05

        def _ln(t, w, b, headc):
            m = jnp.mean(t, axis=-1, keepdims=True)
            d = t - m
            std = jnp.sqrt(jnp.sum(d * d, axis=-1, keepdims=True) / (headc - 1))
            return w * (d / (std + EPS)) + b
        B, N, C = x.shape
        headc = C // HEADS
        qkv = x.reshape(B, N, HEADS, headc).transpose(0, 2, 1, 3)
        k = _ln(qkv, kln_weight, kln_bias, headc)
        v = _ln(qkv, vln_weight, vln_bias, headc)
        kv = jnp.einsum('bhnd,bhne->bhde', k, v) / N
        out = jnp.einsum('bhnd,bhde->bhne', qkv, kv)
        out = out.transpose(0, 2, 1, 3).reshape(B, N, C)
        return out + x

    def _L0_ffn_ref(x, gate_w, gate_b, w1, b1, w2, b2, gamma, beta):
        import jax, jax.numpy as jnp
        import numpy as np
        B, S, H, F, E, K = (8, 256, 256, 512, 16, 2)
        EPS = 1e-05
        gate_logits = x @ gate_w + gate_b
        topk_vals, topk_idx = jax.lax.top_k(gate_logits, K)
        topk_w = jax.nn.softmax(topk_vals, axis=-1)
        h = jax.nn.relu(jnp.einsum('bsh,ehf->bsef', x, w1) + b1)
        expert_out = jnp.einsum('bsef,efh->bseh', h, w2) + b2
        sel = jnp.take_along_axis(expert_out, topk_idx[:, :, :, None], axis=2)
        moe = jnp.sum(topk_w[..., None] * sel, axis=2)
        y = x + moe
        mu = jnp.mean(y, axis=-1, keepdims=True)
        var = jnp.var(y, axis=-1, keepdims=True)
        return (y - mu) / jnp.sqrt(var + EPS) * gamma + beta
    edge_index = jnp.stack([src, dst])
    xn = _layernorm(x, axis=-1)
    x = x + _L0_gnn_ref(xn, edge_index, edge_weight, L0_gnn_W1, L0_gnn_b1, L0_gnn_W2, L0_gnn_b2) + _L0_mix_ref(xn[None], L0_mix_kln_weight, L0_mix_kln_bias, L0_mix_vln_weight, L0_mix_vln_bias)[0]
    x = x + _L0_ffn_ref(_layernorm(x, axis=-1)[None], L0_ffn_gate_w, L0_ffn_gate_b, L0_ffn_w1, L0_ffn_b1, L0_ffn_w2, L0_ffn_b2, L0_ffn_gamma, L0_ffn_beta)[0]
    return x

_drawn_inputs = setup_inputs


def setup_inputs(seed=0):
    import zlib

    import numpy as np

    out = dict(_drawn_inputs(seed))
    spreads = {'L0_mix_kln_weight': (1.0, 0.2),
     'L0_mix_kln_bias': (0.0, 0.473),
     'L0_mix_vln_weight': (1.0, 0.2),
     'L0_mix_vln_bias': (0.0, 0.472),
     'L0_ffn_gate_b': (0.0, 0.474),
     'L0_ffn_b1': (0.0, 0.8),
     'L0_ffn_b2': (0.0, 0.44),
     'L0_ffn_gamma': (1.0, 0.2),
     'L0_ffn_beta': (0.0, 0.328)}
    factors = {'L0_gnn_b1': 8.0, 'L0_gnn_b2': 6.382, 'L0_ffn_w1': 3.706, 'L0_ffn_w2': 2.955}
    for name, (base, spread) in spreads.items():
        noise = np.random.default_rng([zlib.crc32(name.encode()), seed]).standard_normal(out[name].shape)
        drawn = base * np.exp(spread * noise) if base else spread * noise
        out[name] = jnp.asarray(drawn.astype(out[name].dtype))
    for name, factor in factors.items():
        out[name] = (out[name] * factor).astype(out[name].dtype)
    return out
```

```python
from contextlib import ExitStack

import concourse.bass as bass
from concourse import mybir

F32 = mybir.dt.float32
I32 = mybir.dt.int32
U32 = mybir.dt.uint32
U16 = mybir.dt.uint16
BF16 = mybir.dt.bfloat16
ALU = mybir.AluOpType
ACT = mybir.ActivationFunctionType
AX = mybir.AxisListType.X
ds = bass.ds

P = 128
LN_EPS = 1e-5
HEADS = 8


class Steps:

    def __init__(self):
        self.n = 0
        self.shift = 0

    def add(self, k=1):
        self.n += k
        return self.shift + self.n

    def back(self, k):
        return self.shift + (self.n - k)

    def enter(self, rounds_done, per_round):
        self.shift = rounds_done * per_round
        self.at, self.per = self.n, per_round

    def leave(self, rounds):
        assert self.n - self.at == self.per, (self.n - self.at, self.per)
        self.n = self.at + rounds * self.per
        self.shift = 0


def gps_layer(nc, x, src, dst, edge_weight, gW1, gb1, gW2, gb2, klw, klb, vlw, vlb,
              gate_w, gate_b, w1, b1, w2, b2, gamma, beta, out):
    N, D = x.shape
    E = src.shape[0]
    H = gW1.shape[1]
    NX, _, F = w1.shape
    HD = D // HEADS
    DC = D // P
    HC = H // P
    FC = F // P
    TOPK = 2
    NT = -(-N // P)
    TAIL = N - (NT - 1) * P
    GT = 7
    NG = NT // GT
    assert NG * GT == NT and NT % 2 == 1

    CH, SC, QB = 7, 112, 7
    NBUF = 4
    EC = CH * SC
    assert P * EC >= E > (P - 1) * EC and SC % (NBUF * QB) == 0
    EFULL = E // EC
    EREST = E - EFULL * EC
    HALF = 8
    ET = -(-((P * EC + NT * (P - 1)) // P) // (2 * HALF)) * 2 * HALF
    EROUNDS = ET // (2 * HALF)
    REC = 4
    BT = -(-ET // P)
    XT = (TOPK * NT * P + NX * (P - 1)) // P
    XT += (XT % 2)
    NJ = TOPK * NT
    assert XT <= P

    rec_dram = nc.dram_tensor("edge_records_sorted", [P, ET * REC], F32).ap()
    xn_dram = nc.dram_tensor("xn_rows", [NT * P, D], F32).ap()
    x2b_dram = nc.dram_tensor("x2_plus_beta", [P, NT * D], F32).ap()
    bucket_dram = nc.dram_tensor("bucket_of_tile", [BT * P], I32).ap()
    expert_dram = nc.dram_tensor("expert_of_tile", [P], F32).ap()
    experti_dram = nc.dram_tensor("expert_of_tile_int", [P], I32).ap()
    disp_dram = nc.dram_tensor("dispatched_rows", [XT * P, D], F32).ap()
    expout_dram = nc.dram_tensor("expert_rows", [XT * P, D], F32).ap()

    ctx = ExitStack()
    with ctx:
        def sb(name, shape, dt=F32):
            return ctx.enter_context(nc.sbuf_tensor(name, shape, dt))

        def sem(name):
            return ctx.enter_context(nc.semaphore(name))

        bank = [ctx.enter_context(nc.psum_tensor(f"bank{i}", [P, 512], F32)) for i in range(8)]

        xh = sb("xh", [P, NT * D])
        upper = sb("upper", [P, NX * FC * D])
        res = upper[:, 0:NT * D]
        spare = upper[:, NT * D:NX * FC * D]
        lower = sb("lower", [P, NX * DC * F])
        AW = 12 * D + 2 * H
        arena = sb("arena", [P, AW])

        def carver(region, size):
            at = [0]

            def carve(words):
                a = at[0]
                at[0] += words
                assert at[0] <= size, (at[0], size)
                return region[:, a:a + words]
            return carve

        w1_sb = lower[:, :].rearrange("p (e c f) -> p e c f", e=NX, c=DC)
        w2_sb = upper[:, :].rearrange("p (e m d) -> p e m d", e=NX, m=FC)

        carve = carver(lower, NX * DC * F)
        records = carve(EC * REC).rearrange("p (j c) -> p j c", c=REC)
        src_i = carve(EC).bitcast(I32)
        dst_i = carve(EC).bitcast(I32)
        wgt = carve(EC)
        bkt_i = carve(EC).bitcast(I32)
        bkt_f = carve(EC // 2).bitcast(BF16)
        match = [carve(EC // 2).bitcast(BF16) for _ in range(2)]
        masks = [carve(SC // 2).bitcast(U16) for _ in range(4)]
        cums = carve(NT * SC).rearrange("p (b j) -> p b j", b=NT)
        rank = carve(SC)
        slot_i = carve(SC).bitcast(I32)
        tile_i = carve(SC).bitcast(I32)
        row_i = carve(SC).bitcast(I32)
        sq = carve(GT * D)
        kvt = carve(DC * P).rearrange("p (c e) -> p c e", c=DC)
        kvs = carve(DC * P).rearrange("p (c e) -> p c e", c=DC)
        past = carve(BT * NT).rearrange("p (c b) -> p c b", c=BT)
        carve = carver(lower, NX * DC * F)
        sorted_rec = carve(ET * REC).rearrange("p (t c) -> p t c", c=REC)
        edge_rows = carve(2 * HALF * D).rearrange("p (s d) -> p s d", d=D)
        edge_sel = carve(2 * HALF * P).rearrange("p (s n) -> p s n", n=P)
        carve = carver(lower, NX * DC * F)
        exp_rows = carve(GT * TOPK * D).rearrange("p (s d) -> p s d", d=D)
        mixed = carve(GT * D).rearrange("p (s d) -> p s d", d=D)
        normed = carve(GT * D).rearrange("p (s d) -> p s d", d=D)
        x2b_in = carve(GT * D).rearrange("p (s d) -> p s d", d=D)
        out_rows = carve(GT * D).rearrange("p (s d) -> p s d", d=D)
        ZW = XT * D // 8
        zeros = spare[:, 0:ZW]
        assert ET * REC <= ZW <= NX * FC * D - NT * D and XT * D % 8 == 0
        carve = carver(spare, NX * FC * D - NT * D)
        gW1_sb = carve(DC * H).rearrange("p (c f) -> p c f", c=DC)
        gW2_sb = carve(HC * D).rearrange("p (c d) -> p c d", c=HC)
        bucket_row = carve(BT * P).bitcast(I32)[0:1, :]
        carve = carver(arena, AW)
        nd = carve(GT * D)
        kvm = carve(DC * P).rearrange("p (c e) -> p c e", c=DC)
        blockdiag = carve(P)
        vw_row = carve(D)
        vb_row = carve(D)
        xin = [carve(D) for _ in range(2)]
        xT = [carve(D) for _ in range(2)]
        carve = carver(arena, AW)
        hin = [carve(D) for _ in range(2)]
        hT = [carve(D) for _ in range(2)]
        g1 = [carve(H) for _ in range(2)]
        x2 = [carve(D) for _ in range(2)]
        x2b = [carve(D) for _ in range(2)]
        xn2 = [carve(D) for _ in range(2)]
        xn2T = [carve(D) for _ in range(2)]
        carve = carver(upper, NX * FC * D)
        choice = carve(NX * NJ)
        running = carve(NX * NJ)
        restart = carve(NX * NJ)
        past_x = carve(NX)
        disp_rows = arena[:, 0:GT * D].rearrange("p (s d) -> p s d", d=D)
        carve = carver(arena, AW)
        tok = [carve(D) for _ in range(2)]
        tokT = [carve(D) for _ in range(2)]
        hid = [carve(F) for _ in range(2)]
        hidT = [carve(F) for _ in range(2)]
        yrow = [carve(D) for _ in range(2)]
        pick = [carve(P // 2).bitcast(BF16)[0:96, :] for _ in range(2)]

        ident = sb("ident", [P, P])
        ones = sb("ones", [P, P])
        before = sb("before", [P, P])
        iota_n = sb("iota_n", [P, P])
        iota_pc = sb("iota_pc", [P, BT])
        eps_col = sb("eps_col", [P, 1])
        gb1_col = sb("gb1_col", [P, HC])
        gb2_row = sb("gb2_row", [P, D])
        kw_col = sb("kw_col", [P, DC])
        kb_col = sb("kb_col", [P, DC])
        gate_sb = sb("gate_sb", [P, DC, NX])
        gateb_row = sb("gateb_row", [P, NX])
        gamma_row = sb("gamma_row", [P, D])
        beta_row = sb("beta_row", [P, D])
        bias_split = sb("bias_split", [96, F + D], BF16)
        lane_i = sb("lane_i", [96, 1], I32)
        lane32 = sb("lane32", [96, 1])

        cnt = sb("cnt", [P, NT])
        tiles_i = sb("tiles_i", [P, NT], I32)
        tiles_f = sb("tiles_f", [P, NT])
        ends = sb("ends", [P, NT])
        base = sb("base", [P, NT])
        tile_bucket = sb("tile_bucket", [P, BT])
        tile_bucket_i = sb("tile_bucket_i", [P, BT], I32)
        stats = sb("stats", [P, GT, 6])
        mv = sb("mv", [P, GT, 2])
        std = sb("std", [P, GT])
        rstd = sb("rstd", [P, GT])
        hsum = sb("hsum", [P, GT * HEADS])
        hstd = sb("hstd", [P, GT * HEADS])
        hr = sb("hr", [P, GT * HEADS])
        ncol = sb("ncol", [P, DC])
        scat_idx = [sb(f"scat_idx{q}", [P, QB], U32) for q in range(NBUF)]
        scat_rec = [sb(f"scat_rec{q}", [P, QB, REC]) for q in range(NBUF)]
        gath_idx = [sb(f"gath_idx{h}", [P, HALF], U32) for h in range(2)]
        logits = sb("logits", [P, NX])
        top8 = sb("top8", [P, 8])
        idx8 = sb("idx8", [P, 8], U32)
        topv = sb("topv", [P, NJ])
        topi = sb("topi", [P, NJ])
        mix_w = sb("mix_w", [P, NJ])
        gap = sb("gap", [P, NT])
        gap_e = sb("gap_e", [P, NT])
        gap_s = sb("gap_s", [P, NT])
        slot = sb("slot", [P, NJ])
        expert_all = sb("expert_all", [96, P])
        pick_all = sb("pick_all", [96, P], BF16)
        ones_b = sb("ones_b", [96, P], BF16)
        expert_row = sb("expert_row", [1, P], I32)
        st2 = sb("st2", [P, 6])
        mv2 = [sb(f"mv2_{i}", [P, 2]) for i in range(2)]
        std2 = [sb(f"std2_{i}", [P, 1]) for i in range(2)]
        rstd2 = sb("rstd2", [P, 1])
        HA = (GT + 1) // 2
        HALVES = ((0, HA), (HA, GT - HA))
        pair_idx = [sb(f"pair_idx{h}", [P, n * TOPK], U32) for h, (_, n) in enumerate(HALVES)]

        rows_of = lambda a, t0, n: a[t0 * P:(t0 + n) * P, :].rearrange("(t p) d -> p t d", p=P)
        dve_n = Steps()
        s_dve = sem("dve_steps")
        s_apart = sem("waits_apart")

        def looped(n):
            return not isinstance(n, int)

        def tile_bases(dve, nb, totals, earlier):
            dve.tensor_scalar(tiles_i[:, 0:nb], totals, float(P - 1), None, ALU.add).then_inc(s_dve, 1)
            dve.wait_ge(s_dve, dve_n.add())
            dve.tensor_scalar(tiles_i[:, 0:nb], tiles_i[:, 0:nb], 7, None, ALU.arith_shift_right).then_inc(s_dve, 1)
            dve.wait_ge(s_dve, dve_n.add())
            dve.tensor_copy(tiles_f[:, 0:nb], tiles_i[:, 0:nb]).then_inc(s_dve, 1)
            dve.wait_ge(s_dve, dve_n.add())
            dve.tensor_tensor_scan(ends[:, 0:nb], ones[:, 0:nb], tiles_f[:, 0:nb], 0.0, ALU.mult, ALU.add).then_inc(s_dve, 1)
            dve.wait_ge(s_dve, dve_n.add())
            dve.tensor_tensor(base[:, 0:nb], ends[:, 0:nb], tiles_f[:, 0:nb], ALU.subtract).then_inc(s_dve, 1)
            dve.wait_ge(s_dve, dve_n.add())
            dve.scalar_tensor_tensor(base[:, 0:nb], base[:, 0:nb], float(P), earlier, ALU.mult, ALU.add).then_inc(s_dve, 1)
            dve.wait_ge(s_dve, dve_n.add())

        s_emset = sem("edge_pads_cleared")
        s_edges = sem("edges_loaded")
        s_xtail = sem("x_tail_cleared")
        s_x = sem("x_loaded")
        s_par = sem("weights_loaded")
        s_poolc = sem("constants_begun")
        s_consts = sem("constants_made")
        s_ones = sem("ones_made")
        s_zero = sem("zeros_made")
        s_recz = sem("records_zeroed")
        s_dispz = sem("dispatch_zeroed")
        s_bias0 = sem("bias_cleared")
        s_cnt = sem("buckets_counted")
        s_pref = sem("bucket_prefix")
        s_bk = sem("tile_buckets")
        s_bkst = sem("tile_buckets_stored")
        s_bkld = sem("tile_buckets_loaded")
        s_addr = sem("edge_addresses")
        s_stage = [sem(f"scatter_staged{q}") for q in range(NBUF)]
        s_scat = [sem(f"scatter_landed{q}") for q in range(NBUF)]
        s_var = sem("ln1_var")
        s_std = sem("ln1_std")
        s_xn = sem("xn_tiles")
        s_xnst = sem("xn_stored")
        s_dev = sem("heads_centred")
        s_sq = sem("heads_squared")
        s_hss = sem("heads_sumsq")
        s_hstd = sem("heads_std")
        s_nd = sem("heads_normed")
        s_kvmm = sem("kv_products")
        s_kv = sem("kv_matrix")
        s_xin = sem("xn_staged")
        s_xT = sem("xn_transposed")
        s_xTe = sem("xn_transpose_copied")
        s_att = sem("attention_rows")
        s_res = sem("residual_rows")
        QCOLS = NBUF * QB
        QROUNDS = EC // QCOLS
        QPERCH = SC // QCOLS
        bias_f = sq[0:96, 0:F + D]
        bias_r = sq[0:96, F + D:2 * (F + D)]
        assert 2 * (F + D) <= GT * D

        with nc.Block() as block:
            @block.sync
            def _(sp):
                lo = EFULL // 16 * 16
                for n, (tile, a) in enumerate(((src_i, src), (dst_i, dst), (wgt, edge_weight))):
                    sp.wait_ge(s_emset, n + 1)
                    sp.dma_start(tile[0:lo, :], a[0:lo * EC].rearrange("(p j) -> p j", j=EC)).then_inc(s_edges, 16)
                    sp.dma_start(tile[lo:EFULL, :],
                                 a[lo * EC:EFULL * EC].rearrange("(p j) -> p j", j=EC)).then_inc(s_edges, 16)
                    sp.dma_start(tile[EFULL:EFULL + 1, 0:EREST],
                                 a[EFULL * EC:E].rearrange("(p j) -> p j", p=1)).then_inc(s_edges, 16)
                sp.wait_ge(s_zero, 1)
                sp.dma_start(rec_dram, zeros[:, 0:ET * REC]).then_inc(s_recz, 16)
                xv = res.rearrange("p (t d) -> p t d", d=D)
                sp.dma_start(xv[:, 0:NT - 1, :], rows_of(x, 0, NT - 1)).then_inc(s_x, 16)
                sp.wait_ge(s_xtail, 1)
                sp.dma_start(xv[0:TAIL, NT - 1, :], x[(NT - 1) * P:N, :]).then_inc(s_x, 16)

                def row(a):
                    return a.rearrange("(o d) -> o d", o=1).partition_broadcast(P).rearrange("p o d -> p (o d)")

                def flat(a):
                    return a.rearrange("h o d -> (h o d)")

                for to, a in ((gate_sb[:], gate_w.rearrange("(c p) e -> p c e", p=P)),
                              (gb2_row[:], row(gb2)), (vw_row, row(flat(vlw))), (vb_row, row(flat(vlb))),
                              (gateb_row[:], row(gate_b)), (gamma_row[:], row(gamma)), (beta_row[:], row(beta))):
                    sp.dma_start(to, a).then_inc(s_par, 16)
                with nc.allow_non_contiguous_dma(reason="short columns of weights"):
                    for to, a in ((gb1_col, gb1), (kw_col, flat(klw)), (kb_col, flat(klb))):
                        sp.dma_start(to[:], a.rearrange("(c p) -> p c", p=P)).then_inc(s_par, 16)
                sp.wait_ge(s_bias0, 1)
                for q in range(3):
                    sp.dma_start(bias_f[32 * q:32 * q + NX, 0:F], b1).then_inc(s_par, 16)
                    sp.dma_start(bias_f[32 * q:32 * q + NX, F:F + D], b2).then_inc(s_par, 16)
                for k in range(8):
                    sp.dma_start(disp_dram.rearrange("(p r) d -> p (r d)", p=P)[:, k * ZW:(k + 1) * ZW],
                                 zeros).then_inc(s_dispz, 16)
                sp.wait_ge(s_bk, 1)
                with nc.allow_non_contiguous_dma(reason="a column to a row"):
                    sp.dma_start(bucket_dram.rearrange("(c p) -> p c", p=P), tile_bucket_i[:]).then_inc(s_bkst, 16)
                with sp.Fori(0, NG) as g:
                    sp.wait_ge(s_xn, g * GT + GT)
                    sp.dma_start(xn_dram[ds(g * (GT * P), GT * P), :].rearrange("(t p) d -> p t d", p=P),
                                 xh[:, ds(g * (GT * D), GT * D)].rearrange("p (t d) -> p t d", d=D)).then_inc(s_xnst, 16)
                sp.wait_ge(s_xnst, 16 * NG)
                sp.wait_ge(s_dispz, 16 * 8)
                sp.wait_ge(s_bkst, 16)

            @block.gpsimd
            def _(pool):
                pool.memset(ident[:], 0.0).then_inc(s_poolc, 1)
                pool.memset(before[:], 1.0).then_inc(s_poolc, 1)
                pool.iota(iota_n[:], pattern=[[1, P]], base=0, channel_multiplier=0,
                          allow_small_or_imprecise_dtypes=True).then_inc(s_consts, 1)
                pool.iota(iota_pc[:], pattern=[[P, BT]], base=0, channel_multiplier=1,
                          allow_small_or_imprecise_dtypes=True).then_inc(s_consts, 1)
                pool.iota(lane_i[:], pattern=[[0, 1]], base=0, channel_multiplier=1).then_inc(s_consts, 1)
                pool.wait_ge(s_poolc, 2)
                pool.affine_select(out=ident[:], in_=ident[:], compare_op=ALU.not_equal, fill=1.0, base=0,
                                   pattern=[[-1, P]], channel_multiplier=1).then_inc(s_consts, 1)
                pool.affine_select(out=before[:], in_=before[:], compare_op=ALU.is_gt, fill=0.0, base=0,
                                   pattern=[[1, P]], channel_multiplier=-1).then_inc(s_consts, 1)

                def stage(r, q):
                    pool.tensor_copy(scat_idx[q][:], records[:, ds(r * QCOLS + q * QB, QB), 3]).then_inc(s_stage[q], 1)
                    pool.tensor_copy(scat_rec[q][:], records[:, ds(r * QCOLS + q * QB, QB), :]).then_inc(s_stage[q], 1)

                def send(r, q):
                    pool.wait_ge(s_stage[q], r * 2 + 2)
                    pool.sem_inc(s_apart, 1)
                    for c in range(QB):
                        pool.indirect_dma_start(rec_dram.rearrange("p (t c) -> (p t) c", c=REC),
                                                bass.IndirectOffsetOnAxis(scat_idx[q][:, c:c + 1], 0),
                                                scat_rec[q][:, c, :], None).then_inc(s_scat[q], 16)

                pool.wait_ge(s_recz, 16)
                pool.wait_ge(s_addr, 1)
                stage(0, 0)
                for q in range(NBUF):
                    if q + 1 < NBUF:
                        stage(0, q + 1)
                    else:
                        pool.wait_ge(s_scat[0], 16 * QB)
                        stage(1, 0)
                    send(0, q)
                with pool.Fori(1, QROUNDS - 1) as r:
                    pool.wait_ge(s_addr, r + 2)
                    for q in range(NBUF):
                        n, rn = (q + 1, r) if q + 1 < NBUF else (0, r + 1)
                        pool.wait_ge(s_scat[n], rn * (16 * QB))
                        stage(rn, n)
                        send(r, q)
                for q in range(NBUF):
                    if q + 1 < NBUF:
                        pool.wait_ge(s_scat[q + 1], 16 * QB * (QROUNDS - 1))
                        stage(QROUNDS - 1, q + 1)
                    send(QROUNDS - 1, q)
                for q in range(NBUF):
                    pool.wait_ge(s_scat[q], 16 * QB * QROUNDS)

            @block.tensor
            def _(pe):
                pe.wait_ge(s_ones, 1)
                pe.wait_ge(s_consts, 5)
                pe.wait_ge(s_cnt, NT)
                pe.matmul(bank[0][:, 0:NT], ones[:], cnt[:], start=True, stop=True).then_inc(s_pref, 1)
                pe.matmul(bank[1][:, 0:NT], before[:], cnt[:], start=True, stop=True).then_inc(s_pref, 1)

                def sums(g):
                    pe.wait_ge(s_nd, g + 1)
                    for k in range(GT):
                        first = not looped(g) and g == 0 and k == 0
                        last = not looped(g) and g == NG - 1 and k == GT - 1
                        for c in range(DC):
                            a = nd[:, k * D + c * P:k * D + (c + 1) * P]
                            pe.matmul(bank[2 + c][:, 0:P], a, a, start=first, stop=last)
                            pe.matmul(bank[4 + c][:, 0:1], a, ones[:, 0:1], start=first, stop=last)
                        mm = pe.matmul(bank[6][:, 0:D], ones[:], nd[:, k * D:(k + 1) * D], start=first, stop=last)
                    mm.then_inc(s_kvmm, 1)

                sums(0)
                with pe.Fori(1, NG - 1) as g:
                    sums(g)
                sums(NG - 1)

                def turn(t, p):
                    pe.wait_ge(s_xin, t + 1)
                    for c in range(DC):
                        mm = pe.transpose(bank[p][:, c * P:(c + 1) * P], xin[p][:, c * P:(c + 1) * P], ident[:])
                    mm.then_inc(s_xT, 1)

                def attend(t, p):
                    pe.wait_ge(s_xTe, t + 1)
                    for c in range(DC):
                        mm = pe.matmul(bank[2 + p][:, c * P:(c + 1) * P], xT[p][:, c * P:(c + 1) * P], kvm[:, c, :],
                                       start=True, stop=True)
                    mm.then_inc(s_att, 1)

                def step(t, p):
                    turn(t, p)
                    if looped(t) or t >= 1:
                        if looped(t) or t >= 3:
                            pe.wait_ge(s_res, t - 2)
                        attend(t - 1, 1 - p)

                pe.wait_ge(s_kv, 1)
                for t in range(3):
                    step(t, t % 2)
                with pe.Fori(0, (NT - 3) // 2) as j:
                    step(j * 2 + 3, 1)
                    step(j * 2 + 4, 0)
                pe.wait_ge(s_res, NT - 2)
                attend(NT - 1, (NT - 1) % 2)

            @block.scalar
            def _(act):
                with act.Fori(0, NG) as g:
                    act.wait_ge(s_var, g * GT + GT)
                    act.activation(std[:], mv[:, :, 1], ACT.Sqrt, bias=eps_col[:]).then_inc(s_std, 1)
                with act.Fori(0, NG) as g:
                    act.wait_ge(s_dev, g + 1)
                    act.activation(sq, nd, ACT.Square).then_inc(s_sq, 1)
                    act.wait_ge(s_hss, g + 1)
                    act.activation(hstd[:], hsum[:], ACT.Sqrt, scale=1.0 / (HD - 1)).then_inc(s_hstd, 1)

                def step(t, p):
                    if looped(t) or t < NT:
                        if looped(t) or t >= 2:
                            act.wait_ge(s_xT, t - 1)
                        act.activation(xin[p], xh[:, ds(t * D, D)], ACT.Copy).then_inc(s_xin, 1)
                    if looped(t) or t >= 1:
                        act.wait_ge(s_xT, t)
                        if looped(t) or t >= 3:
                            act.wait_ge(s_att, t - 2)
                        act.activation(xT[1 - p], bank[1 - p][:, 0:D], ACT.Copy).then_inc(s_xTe, 1)

                act.wait_ge(s_kv, 1)
                for t in range(3):
                    step(t, t % 2)
                with act.Fori(0, (NT - 3) // 2) as j:
                    step(j * 2 + 3, 1)
                    step(j * 2 + 4, 0)
                step(NT, NT % 2)

            @block.vector
            def _(dve):
                n = dve_n
                dve.memset(src_i, 0).then_inc(s_emset, 1)
                dve.memset(dst_i, 0).then_inc(s_emset, 1)
                dve.memset(wgt, 0.0).then_inc(s_emset, 1)
                dve.memset(zeros, 0.0).then_inc(s_zero, 1)
                dve.memset(ones[:], 1.0).then_inc(s_ones, 1)
                dve.memset(res[:, (NT - 1) * D:NT * D], 0.0).then_inc(s_xtail, 1)
                dve.memset(bias_f, 0.0).then_inc(s_bias0, 1)
                dve.memset(eps_col[:], LN_EPS).then_inc(s_dve, 1)
                dve.memset(ones_b[:], 1.0).then_inc(s_dve, 1)
                dve.memset(blockdiag, 0.0).then_inc(s_dve, 1)
                dve.wait_ge(s_dve, n.add(3))
                for q in range(P // HD):
                    dve.memset(blockdiag[q * HD:(q + 1) * HD, q * HD:(q + 1) * HD], 1.0 / N).then_inc(s_dve, 1)
                dve.wait_ge(s_edges, 16 * 9)
                dve.tensor_scalar(bkt_i, src_i, 7, None, ALU.arith_shift_right).then_inc(s_dve, 1)
                dve.wait_ge(s_dve, n.add(P // HD + 1))
                dve.tensor_copy(bkt_f, bkt_i).then_inc(s_dve, 1)
                dve.wait_ge(s_dve, n.add())
                dve.wait_ge(s_consts, 5)
                with dve.Fori(0, NT // GT) as r:
                    for k in range(GT):
                        if k >= 2:
                            dve.wait_ge(s_cnt, r * GT + k - 1)
                        dve.tensor_scalar(match[k % 2], bkt_f, iota_n[:, ds(r * GT + k, 1)], 0.0, ALU.is_equal, ALU.add,
                                          accum_out=cnt[:, ds(r * GT + k, 1)]).then_inc(s_cnt, 1)
                    dve.wait_ge(s_cnt, r * GT + GT)
                dve.tensor_copy(records[:, :, 0], dst_i).then_inc(s_dve, 1)
                dve.tensor_scalar(bkt_i, src_i, P - 1, None, ALU.bitwise_and).then_inc(s_dve, 1)
                dve.tensor_copy(records[:, :, 2], wgt).then_inc(s_dve, 1)
                dve.wait_ge(s_dve, n.add(3))
                dve.tensor_copy(records[:, :, 1], bkt_i).then_inc(s_dve, 1)
                dve.wait_ge(s_dve, n.add())
                dve.wait_ge(s_pref, 2)
                tile_bases(dve, NT, bank[0][:, 0:NT], bank[1][:, 0:NT])
                dve.tensor_copy(cums[:, :, SC - 1], base[:]).then_inc(s_dve, 1)
                dve.wait_ge(s_dve, n.add())

                per_chunk = 3 * NT + 4
                with dve.Fori(0, CH) as ch:
                    n.enter(ch, per_chunk)
                    for b in range(NT + 2):
                        if b < NT:
                            dve.wait_ge(s_dve, n.back(2))
                            dve.tensor_scalar(masks[b % 4], bkt_f[:, ds(ch * SC, SC)], float(b), None,
                                              ALU.is_equal).then_inc(s_dve, 1)
                            n.add()
                        if 1 <= b <= NT:
                            dve.wait_ge(s_dve, n.back(1 if b < NT else 0))
                            dve.tensor_tensor_scan(cums[:, b - 1, :], ones[:, 0:SC], masks[(b - 1) % 4],
                                                   cums[:, b - 1, SC - 1:SC], ALU.mult, ALU.add).then_inc(s_dve, 1)
                            n.add()
                        if b >= 2:
                            if b > NT:
                                dve.wait_ge(s_dve, n.back(0))
                                dve.sem_inc(s_apart, 1)
                            dve.copy_predicated(rank, masks[(b - 2) % 4], cums[:, b - 2, :]).then_inc(s_dve, 1)
                            n.add()
                    dve.wait_ge(s_dve, n.back(0))
                    dve.tensor_scalar(slot_i, rank, -1.0, None, ALU.add).then_inc(s_dve, 1)
                    dve.wait_ge(s_dve, n.add())
                    dve.tensor_scalar(tile_i, slot_i, 7, None, ALU.arith_shift_right).then_inc(s_dve, 1)
                    dve.tensor_scalar(row_i, slot_i, P - 1, None, ALU.bitwise_and).then_inc(s_dve, 1)
                    dve.wait_ge(s_dve, n.add(2))
                    dve.scalar_tensor_tensor(rank, row_i, float(ET), tile_i, ALU.mult, ALU.add).then_inc(s_dve, 1)
                    dve.wait_ge(s_dve, n.add())
                    dve.tensor_copy(records[:, ds(ch * SC, SC), 3], rank).then_inc(s_addr, QPERCH)
                    dve.wait_ge(s_addr, ch * QPERCH + QPERCH)
                    n.leave(CH)

                dve.tensor_tensor(past, iota_pc[:].unsqueeze(2).to_broadcast([P, BT, NT]),
                                  ends[:].unsqueeze(1).to_broadcast([P, BT, NT]), ALU.is_ge).then_inc(s_dve, 1)
                dve.wait_ge(s_dve, n.add())
                dve.tensor_reduce(tile_bucket[:], past, AX, ALU.add).then_inc(s_dve, 1)
                dve.wait_ge(s_dve, n.add())
                dve.tensor_scalar(tile_bucket_i[:], tile_bucket[:], float(NT - 1), None, ALU.min).then_inc(s_bk, 1)

                dve.wait_ge(s_par, 16 * 16)
                thirds = [slice(32 * q, 32 * q + 32) for q in range(3)]
                for q in range(3):
                    for rows in thirds[q:]:
                        dve.tensor_copy(bias_split[rows, :], bias_f[rows, :]).then_inc(s_dve, 1)
                    dve.wait_ge(s_dve, n.add(3 - q))
                    if q < 2:
                        for rows in thirds[q + 1:]:
                            dve.tensor_copy(bias_r[rows, :], bias_split[rows, :]).then_inc(s_dve, 1)
                        dve.wait_ge(s_dve, n.add(2 - q))
                        for rows in thirds[q + 1:]:
                            dve.tensor_tensor(bias_f[rows, :], bias_f[rows, :], bias_r[rows, :],
                                              ALU.subtract).then_inc(s_dve, 1)
                        dve.wait_ge(s_dve, n.add(2 - q))

                dve.wait_ge(s_x, 32)
                with dve.Fori(0, NG) as g:
                    n.enter(g, GT + 1)
                    for k in range(GT):
                        dve.bn_stats(stats[:, k, :], res[:, ds(g * (GT * D) + k * D, D)]).then_inc(s_dve, 1)
                    dve.wait_ge(s_dve, n.add(GT))
                    dve.sem_inc(s_apart, 1)
                    for k in range(GT):
                        dve.bn_aggr(mv[:, k, :], stats[:, k, :]).then_inc(s_var, 1)
                    dve.wait_ge(s_std, g + 1)
                    dve.reciprocal(rstd[:], std[:]).then_inc(s_dve, 1)
                    dve.wait_ge(s_dve, n.add())
                    for k in range(GT):
                        at = ds(g * (GT * D) + k * D, D)
                        dve.tensor_scalar(xh[:, at], res[:, at], mv[:, k, 0:1], rstd[:, k:k + 1],
                                          ALU.subtract, ALU.mult).then_inc(s_xn, 1)
                    dve.wait_ge(s_xn, g * GT + GT)
                    n.leave(NG)

                def heads(g):
                    at = ds(g * (GT * D), GT * D)
                    hv = xh[:, at].rearrange("p (h e) -> p h e", e=HD)
                    ndh = nd.rearrange("p (h e) -> p h e", e=HD)
                    wide = lambda a: a[:].unsqueeze(2).to_broadcast([P, GT * HEADS, HD])
                    dve.tensor_reduce(hsum[:], hv, AX, ALU.add).then_inc(s_dve, 1)
                    dve.wait_ge(s_dve, n.add())
                    dve.tensor_scalar(hsum[:], hsum[:], 1.0 / HD, None, ALU.mult).then_inc(s_dve, 1)
                    dve.wait_ge(s_dve, n.add())
                    if looped(g) or g >= 1:
                        dve.wait_ge(s_kvmm, g)
                    dve.tensor_tensor(ndh, hv, wide(hsum), ALU.subtract).then_inc(s_dev, 1)
                    rv = res[:, at].rearrange("p (t d) -> p t d", d=D)
                    dve.tensor_tensor(rv, rv, gb2_row[:].unsqueeze(1).to_broadcast([P, GT, D]), ALU.add).then_inc(s_dve, 1)
                    dve.wait_ge(s_dve, n.add())
                    dve.wait_ge(s_sq, g + 1)
                    dve.tensor_reduce(hsum[:], sq.rearrange("p (h e) -> p h e", e=HD), AX, ALU.add).then_inc(s_hss, 1)
                    dve.wait_ge(s_hstd, g + 1)
                    dve.tensor_scalar(hr[:], hstd[:], LN_EPS, None, ALU.add).then_inc(s_dve, 1)
                    dve.wait_ge(s_dve, n.add())
                    dve.reciprocal(hr[:], hr[:]).then_inc(s_dve, 1)
                    dve.wait_ge(s_dve, n.add())
                    dve.tensor_tensor(ndh, ndh, wide(hr), ALU.mult).then_inc(s_nd, 1)
                    dve.wait_ge(s_nd, g + 1)

                at0 = n.n
                heads(0)
                per_group = n.n - at0
                with dve.Fori(1, NG) as g:
                    n.enter(g - 1, per_group)
                    heads(g)
                    n.leave(NG - 1)

                dve.wait_ge(s_kvmm, NG)
                for c in range(DC):
                    cols = slice(c * P, (c + 1) * P)
                    dve.tensor_copy(ncol[:, c:c + 1], bank[4 + c][:, 0:1]).then_inc(s_dve, 1)
                    dve.tensor_tensor(kvt[:, c, :], bank[2 + c][:, 0:P], vw_row[:, cols], ALU.mult).then_inc(s_dve, 1)
                    dve.tensor_tensor(kvs[:, c, :], bank[6][:, cols], vw_row[:, cols], ALU.mult).then_inc(s_dve, 1)
                    dve.wait_ge(s_dve, n.add(3))
                    dve.scalar_tensor_tensor(kvt[:, c, :], vb_row[:, cols], ncol[:, c:c + 1], kvt[:, c, :],
                                             ALU.mult, ALU.add).then_inc(s_dve, 1)
                    dve.scalar_tensor_tensor(kvs[:, c, :], vb_row[:, cols], float(N), kvs[:, c, :],
                                             ALU.mult, ALU.add).then_inc(s_dve, 1)
                    dve.wait_ge(s_dve, n.add(2))
                    dve.tensor_scalar(kvt[:, c, :], kvt[:, c, :], kw_col[:, c:c + 1], None, ALU.mult).then_inc(s_dve, 1)
                    dve.wait_ge(s_dve, n.add())
                    dve.scalar_tensor_tensor(kvt[:, c, :], kvs[:, c, :], kb_col[:, c:c + 1], kvt[:, c, :],
                                             ALU.mult, ALU.add).then_inc(s_dve, 1)
                    dve.wait_ge(s_dve, n.add())
                    dve.tensor_tensor(kvt[:, c, :], kvt[:, c, :], blockdiag, ALU.mult).then_inc(s_dve, 1)
                    dve.wait_ge(s_dve, n.add())
                    dve.tensor_tensor(kvm[:, c, :], kvt[:, c, :], ident[:], ALU.add).then_inc(s_dve, 1)
                    dve.wait_ge(s_dve, n.add())
                dve.tensor_scalar(lane_i[:], lane_i[:], 31, None, ALU.bitwise_and).then_inc(s_kv, 1)
                dve.wait_ge(s_kv, 1)
                dve.tensor_copy(lane32[:], lane_i[:]).then_inc(s_dve, 1)
                dve.wait_ge(s_dve, n.add())

                def residual(t, p):
                    dve.wait_ge(s_att, t + 1)
                    at = ds(t * D, D)
                    dve.tensor_tensor(res[:, at], res[:, at], bank[2 + p][:, 0:D], ALU.add).then_inc(s_res, 1)

                residual(0, 0)
                with dve.Fori(0, (NT - 1) // 2) as j:
                    residual(j * 2 + 1, 1)
                    residual(j * 2 + 2, 0)

        s_srec = sem("sorted_records_loaded")
        s_gw = sem("gin_weights_loaded")
        s_gst = [sem(f"gather_staged{h}") for h in range(2)]
        s_gath = [sem(f"edge_rows_landed{i}") for i in range(2 * HALF)]
        s_sel = sem("edge_matrix_built")
        s_sum = sem("edge_sums")
        s_acc = sem("edge_sums_added")
        ROUND = 2 * HALF
        SUMB = 4

        with nc.Block() as block:
            @block.sync
            def _(sp):
                sp.dma_start(sorted_rec.rearrange("p t c -> p (t c)"), rec_dram).then_inc(s_srec, 16)
                sp.dma_start(bucket_row, bucket_dram.rearrange("(o t) -> o t", o=1)).then_inc(s_bkld, 16)
                sp.dma_start(gW1_sb, gW1.rearrange("(c p) f -> p c f", p=P)).then_inc(s_gw, 16)
                sp.dma_start(gW2_sb, gW2.rearrange("(c p) d -> p c d", p=P)).then_inc(s_gw, 16)

            @block.scalar
            def _(act):
                def stage(r):
                    for h in range(2):
                        if looped(r):
                            act.wait_ge(s_sum, r * ROUND + (h - 1) * HALF)
                        act.activation(gath_idx[h][:], sorted_rec[:, ds(r * ROUND + h * HALF, HALF), 0],
                                       ACT.Copy).then_inc(s_gst[h], 1)

                act.wait_ge(s_srec, 16)
                stage(0)
                with act.Fori(1, EROUNDS) as r:
                    stage(r)

            @block.gpsimd
            def _(pool):
                with pool.Fori(0, EROUNDS) as r:
                    for h in range(2):
                        pool.wait_ge(s_gst[h], r + 1)
                        pool.sem_inc(s_apart, 1)
                        for c in range(HALF):
                            pool.indirect_dma_start(edge_rows[:, h * HALF + c, :], None, xn_dram,
                                                    bass.IndirectOffsetOnAxis(gath_idx[h][:, c:c + 1], 0)
                                                    ).then_inc(s_gath[h * HALF + c], 16)

            @block.tensor
            def _(pe):
                def sums(r):
                    for c in range(ROUND):
                        pe.wait_ge(s_sel, r * ROUND + c + 1)
                        pe.wait_ge(s_gath[c], r * 16 + 16)
                        if looped(r) or c >= SUMB:
                            pe.wait_ge(s_acc, r * ROUND + c + 1 - SUMB)
                        pe.matmul(bank[c % SUMB][:, 0:D], edge_sel[:, c, :], edge_rows[:, c, :],
                                  start=True, stop=True).then_inc(s_sum, 1)

                sums(0)
                with pe.Fori(1, EROUNDS) as r:
                    sums(r)

            @block.vector
            def _(dve):
                def build(r, h):
                    for c in range(HALF):
                        t = r * ROUND + h * HALF + c
                        dve.tensor_scalar(edge_sel[:, h * HALF + c, :], iota_n[:], sorted_rec[:, ds(t, 1), 1],
                                          sorted_rec[:, ds(t, 1), 2], ALU.is_equal, ALU.mult).then_inc(s_sel, 1)

                def add(r, h):
                    _, buckets = nc.values_load_multi_w_load_instructions(
                        bucket_row[0:1, ds(r * ROUND + h * HALF, HALF)], engines=(nc.vector.engine,),
                        min_val=0, max_val=NT - 1)
                    for c in range(HALF):
                        t = r * ROUND + h * HALF + c
                        dve.wait_ge(s_sum, t + 1)
                        if looped(r) or h or c:
                            dve.wait_ge(s_acc, t)
                        at = ds(buckets[c] * D, D)
                        dve.tensor_tensor(xh[:, at], xh[:, at], bank[(h * HALF + c) % SUMB][:, 0:D],
                                          ALU.add).then_inc(s_acc, 1)

                dve.wait_ge(s_srec, 16)
                build(0, 0)
                build(0, 1)
                dve.wait_ge(s_bkld, 16)
                add(0, 0)
                with dve.Fori(1, EROUNDS) as r:
                    dve.wait_ge(s_acc, r * ROUND - HALF)
                    build(r, 0)
                    add(r - 1, 1)
                    dve.wait_ge(s_acc, r * ROUND)
                    build(r, 1)
                    add(r, 0)
                add(EROUNDS - 1, 1)

        s_w1 = sem("w1_loaded")
        s_hin = sem("h_staged")
        s_hT = sem("h_transposed")
        s_hTe = sem("h_transpose_copied")
        s_g = sem("hidden_sums")
        s_gr = sem("hidden_rows")
        s_o = sem("mlp_rows")
        s_x2 = sem("x2_rows")
        s_x2b = sem("x2_plus_beta_rows")
        s_x2st = [sem(f"x2_stored{i}") for i in range(2)]
        s_var2 = sem("ln2_var")
        s_std2 = sem("ln2_std")
        s_xn2 = sem("xn2_rows")
        s_xn2k = sem("xn2_kept")
        s_x2T = sem("xn2_transposed")
        s_x2Te = sem("xn2_transpose_copied")
        s_l = sem("gate_sums")
        s_lg = sem("logits")

        def tile_at(j, k):
            return j * 2 + k, k % 2, j + k // 2

        def has(t):
            return looped(t) or 0 <= t < NT

        def over(v):
            return looped(v) or v > 0

        def run_steps(eng, step, first, last, j0, j1):
            for k in range(first, 2 * j0):
                step(0, k)
            with eng.Fori(j0, j1) as j:
                step(j, 0)
                step(j, 1)
            for k in range(2 * j1, last + 1):
                step(0, k)

        C_STEPS = (-2, NT + 2, 2, (NT - 3) // 2)

        with nc.Block() as block:
            @block.sync
            def _(sp):
                sp.dma_start(w1_sb, w1.rearrange("e (c p) f -> p e c f", p=P)).then_inc(s_w1, 16)

                def step(j, k):
                    t, p, half = tile_at(j, k)
                    sp.wait_ge(s_x2b, t + 1)
                    sp.dma_start(x2b_dram[:, ds(t * D, D)], x2b[p]).then_inc(s_x2st[p], 16)

                run_steps(sp, step, 0, NT - 1, 2, (NT - 3) // 2)
                for p in range(2):
                    sp.wait_ge(s_x2st[p], 16 * ((NT + 1 - p) // 2))

            @block.tensor
            def _(pe):
                pe.wait_ge(s_gw, 32)

                def step(j, k):
                    t, p, _ = tile_at(j, k)
                    if has(t):
                        pe.wait_ge(s_hTe, t + 1)
                        if over(t - 1):
                            pe.wait_ge(s_gr, (t - 1) * HC)
                        for m in range(HC):
                            for c in range(DC):
                                mm = pe.matmul(bank[2 + p][:, m * P:(m + 1) * P], gW1_sb[:, c, m * P:(m + 1) * P],
                                               hT[p][:, c * P:(c + 1) * P], start=c == 0, stop=c == DC - 1)
                        mm.then_inc(s_g, 1)
                    t, p, _ = tile_at(j, k + 1)
                    if has(t):
                        pe.wait_ge(s_hin, t + 1)
                        if over(t - 1):
                            pe.wait_ge(s_hTe, t - 1)
                        for c in range(DC):
                            mm = pe.transpose(bank[p][:, c * P:(c + 1) * P], hin[p][:, c * P:(c + 1) * P], ident[:])
                        mm.then_inc(s_hT, 1)
                    t, p, _ = tile_at(j, k - 1)
                    if has(t):
                        pe.wait_ge(s_gr, t * HC + HC)
                        if over(t - 1):
                            pe.wait_ge(s_x2, t - 1)
                        for m in range(HC):
                            mm = pe.matmul(bank[4 + p][:, 0:D], g1[p][:, m * P:(m + 1) * P], gW2_sb[:, m, :],
                                           start=m == 0, stop=m == HC - 1)
                        mm.then_inc(s_o, 1)
                    t, p, _ = tile_at(j, k - 2)
                    if has(t):
                        pe.wait_ge(s_xn2, t + 1)
                        if over(t):
                            pe.wait_ge(s_x2Te, t)
                        for c in range(DC):
                            mm = pe.transpose(bank[6][:, c * P:(c + 1) * P], xn2[p][:, c * P:(c + 1) * P], ident[:])
                        mm.then_inc(s_x2T, 1)
                    t, p, _ = tile_at(j, k - 3)
                    if has(t):
                        pe.wait_ge(s_x2Te, t + 1)
                        if over(t):
                            pe.wait_ge(s_lg, t)
                        for c in range(DC):
                            mm = pe.matmul(bank[7][:, 0:NX], xn2T[p][:, c * P:(c + 1) * P], gate_sb[:, c, :],
                                           start=c == 0, stop=c == DC - 1)
                        mm.then_inc(s_l, 1)

                run_steps(pe, step, *C_STEPS)

            @block.scalar
            def _(act):
                def step(j, k):
                    t, p, _ = tile_at(j, k)
                    if has(t):
                        act.wait_ge(s_g, t + 1)
                        if over(t - 1):
                            act.wait_ge(s_o, t - 1)
                        for m in range(HC):
                            act.activation(g1[p][:, m * P:(m + 1) * P], bank[2 + p][:, m * P:(m + 1) * P], ACT.Relu,
                                           bias=gb1_col[:, m:m + 1]).then_inc(s_gr, 1)
                    t, p, _ = tile_at(j, k + 1)
                    if has(t):
                        act.wait_ge(s_hT, t + 1)
                        if over(t - 1):
                            act.wait_ge(s_g, t - 1)
                        act.activation(hT[p], bank[p][:, 0:D], ACT.Copy).then_inc(s_hTe, 1)
                    t, p, _ = tile_at(j, k + 2)
                    if has(t):
                        if over(t - 1):
                            act.wait_ge(s_hT, t - 1)
                        act.activation(hin[p], xh[:, ds(t * D, D)], ACT.Copy).then_inc(s_hin, 1)
                    t, p, _ = tile_at(j, k - 1)
                    if has(t):
                        act.wait_ge(s_var2, t + 1)
                        act.activation(std2[p][:], mv2[p][:, 1:2], ACT.Sqrt, bias=eps_col[:]).then_inc(s_std2, 1)
                    t, p, _ = tile_at(j, k - 2)
                    if has(t):
                        act.wait_ge(s_x2T, t + 1)
                        if over(t - 1):
                            act.wait_ge(s_l, t - 1)
                        act.activation(xn2T[p], bank[6][:, 0:D], ACT.Copy).then_inc(s_x2Te, 1)
                        act.activation(xh[:, ds(t * D, D)], xn2[p], ACT.Copy).then_inc(s_xn2k, 1)

                run_steps(act, step, *C_STEPS)

            @block.vector
            def _(dve):
                n = dve_n

                def step(j, k):
                    t, p, half = tile_at(j, k - 1)
                    t3, _, _ = tile_at(j, k - 3)
                    if has(t):
                        dve.wait_ge(s_o, t + 1)
                        if over(t - 1):
                            dve.wait_ge(s_xn2k, t - 1)
                        dve.tensor_tensor(x2[p], res[:, ds(t * D, D)], bank[4 + p][:, 0:D], ALU.add).then_inc(s_x2, 1)
                    if has(t3):
                        dve.wait_ge(s_l, t3 + 1)
                        dve.tensor_tensor(logits[:], bank[7][:, 0:NX], gateb_row[:], ALU.add).then_inc(s_lg, 1)
                    if has(t):
                        dve.wait_ge(s_x2, t + 1)
                        dve.bn_stats(st2[:], x2[p]).then_inc(s_dve, 1)
                        n.add()
                    if has(t3):
                        dve.wait_ge(s_lg, t3 + 1)
                        dve.sem_inc(s_apart, 1)
                        dve.max(top8[:], logits[:]).then_inc(s_dve, 1)
                        n.add()
                    if has(t):
                        dve.wait_ge(s_dve, n.back(1 if has(t3) else 0))
                        dve.sem_inc(s_apart, 1)
                        dve.bn_aggr(mv2[p][:], st2[:]).then_inc(s_var2, 1)
                        if over(half):
                            dve.wait_ge(s_x2st[p], half * 16)
                        dve.tensor_tensor(x2b[p], x2[p], beta_row[:], ALU.add).then_inc(s_x2b, 1)
                    if has(t3):
                        dve.wait_ge(s_dve, n.back(0))
                        dve.sem_inc(s_apart, 1)
                        dve.max_index(idx8[:], top8[:], logits[:]).then_inc(s_dve, 1)
                        dve.tensor_copy(topv[:, ds(t3 * TOPK, TOPK)], top8[:, 0:TOPK]).then_inc(s_dve, 1)
                        n.add(2)
                    if has(t):
                        dve.wait_ge(s_std2, t + 1)
                        dve.reciprocal(rstd2[:], std2[p][:]).then_inc(s_dve, 1)
                        n.add()
                    if has(t3):
                        dve.wait_ge(s_dve, n.back(2 if has(t) else 1))
                        dve.tensor_copy(topi[:, ds(t3 * TOPK, TOPK)], idx8[:, 0:TOPK]).then_inc(s_dve, 1)
                        n.add()
                    dve.wait_ge(s_dve, n.back(0))
                    if has(t):
                        dve.tensor_scalar(xn2[p], x2[p], mv2[p][:, 0:1], rstd2[:], ALU.subtract, ALU.mult).then_inc(s_xn2, 1)
                        dve.wait_ge(s_xn2, t + 1)

                first, last, j0, j1 = C_STEPS
                for k in range(first, 2 * j0):
                    step(0, k)
                with dve.Fori(j0, j1) as j:
                    n.enter(j - j0, 2 * 6)
                    step(j, 0)
                    step(j, 1)
                    n.leave(j1 - j0)
                for k in range(2 * j1, last + 1):
                    step(0, k)

        s_w2 = sem("w2_loaded")
        s_gap = sem("gate_gaps")
        s_gape = sem("gate_exps")
        s_xcnt = sem("experts_counted")
        s_xpref = sem("expert_prefix")
        s_te = sem("tile_experts")
        s_test = sem("tile_experts_stored")
        s_teld = sem("tile_experts_loaded")
        s_slot = sem("slots")
        s_pst = [sem(f"dispatch_staged{h}") for h in range(2)]
        s_disp = [sem(f"dispatch_landed{h}") for h in range(2)]
        s_pick = sem("bias_picks")

        with nc.Block() as block:
            @block.sync
            def _(sp):
                sp.wait_ge(s_te, 2)
                with nc.allow_non_contiguous_dma(reason="a column to a row"):
                    sp.dma_start(expert_dram.rearrange("(p o) -> p o", o=1), tile_bucket[:, 0:1]).then_inc(s_test, 16)
                    sp.dma_start(experti_dram.rearrange("(p o) -> p o", o=1), tile_bucket_i[:, 0:1]).then_inc(s_test, 16)
                sp.wait_ge(s_test, 32)
                sp.dma_start(expert_all[:], expert_dram.rearrange("(o t) -> o t", o=1).partition_broadcast(96)
                             .rearrange("p o t -> p (o t)")).then_inc(s_teld, 16)
                sp.dma_start(expert_row[:], experti_dram.rearrange("(o t) -> o t", o=1)).then_inc(s_teld, 16)
                sp.wait_ge(s_slot, 1)
                sp.dma_start(w2_sb, w2.rearrange("e (m p) d -> p e m d", p=P)).then_inc(s_w2, 16)

            @block.tensor
            def _(pe):
                pe.wait_ge(s_xcnt, 1)
                pe.matmul(bank[0][:, 0:NX], ones[:], cnt[:, 0:NX], start=True, stop=True).then_inc(s_xpref, 1)
                pe.matmul(bank[1][:, 0:NX], before[:], cnt[:, 0:NX], start=True, stop=True).then_inc(s_xpref, 1)

            @block.vector
            def _(dve):
                n = dve_n
                cv = choice.rearrange("p (e j) -> p e j", e=NX)
                rv = running.rearrange("p (e j) -> p e j", e=NX)
                tv = topv[:].rearrange("p (t k) -> p t k", k=TOPK)
                mw = mix_w[:].rearrange("p (t k) -> p t k", k=TOPK)
                dve.tensor_tensor(gap[:], tv[:, :, 1], tv[:, :, 0], ALU.subtract).then_inc(s_gap, 1)
                dve.tensor_tensor(cv, topi[:].unsqueeze(1).to_broadcast([P, NX, NJ]),
                                  iota_n[:, 0:NX].unsqueeze(2).to_broadcast([P, NX, NJ]), ALU.is_equal).then_inc(s_dve, 1)
                dve.memset(restart, 1.0).then_inc(s_dve, 1)
                dve.wait_ge(s_dve, n.add(2))
                dve.tensor_reduce(cnt[:, 0:NX], cv, AX, ALU.add).then_inc(s_xcnt, 1)
                dve.memset(restart.rearrange("p (e j) -> p e j", e=NX)[:, :, 0:1], 0.0).then_inc(s_dve, 1)
                dve.wait_ge(s_dve, n.add())
                dve.tensor_tensor_scan(running, restart, choice, 0.0, ALU.mult, ALU.add).then_inc(s_dve, 1)
                dve.wait_ge(s_dve, n.add())
                dve.wait_ge(s_xpref, 2)
                tile_bases(dve, NX, bank[0][:, 0:NX], bank[1][:, 0:NX])
                dve.tensor_tensor(past_x, iota_pc[:, 0:1].to_broadcast([P, NX]), ends[:, 0:NX],
                                  ALU.is_ge).then_inc(s_dve, 1)
                dve.wait_ge(s_dve, n.add())
                dve.tensor_reduce(tile_bucket[:, 0:1], past_x, AX, ALU.add).then_inc(s_dve, 1)
                dve.wait_ge(s_dve, n.add())
                dve.tensor_scalar(tile_bucket[:, 0:1], tile_bucket[:, 0:1], float(NX - 1), None, ALU.min).then_inc(s_te, 1)
                dve.wait_ge(s_te, 1)
                dve.tensor_copy(tile_bucket_i[:, 0:1], tile_bucket[:, 0:1]).then_inc(s_te, 1)
                dve.tensor_tensor(rv, rv, base[:, 0:NX].unsqueeze(2).to_broadcast([P, NX, NJ]), ALU.add).then_inc(s_dve, 1)
                dve.wait_ge(s_dve, n.add())
                dve.tensor_tensor(running, running, choice, ALU.mult).then_inc(s_dve, 1)
                dve.wait_ge(s_dve, n.add())
                dve.tensor_reduce(slot[:], running.rearrange("p (e j) -> p j e", e=NX), AX, ALU.add).then_inc(s_dve, 1)
                dve.wait_ge(s_dve, n.add())
                dve.tensor_scalar(slot[:], slot[:], -1.0, None, ALU.add).then_inc(s_slot, 1)
                dve.wait_ge(s_gape, 1)
                dve.tensor_scalar(gap_s[:], gap_e[:], 1.0, None, ALU.add).then_inc(s_dve, 1)
                dve.wait_ge(s_dve, n.add())
                dve.reciprocal(gap_s[:], gap_s[:]).then_inc(s_dve, 1)
                dve.wait_ge(s_dve, n.add())
                dve.tensor_copy(mw[:, :, 0], gap_s[:]).then_inc(s_dve, 1)
                dve.tensor_tensor(mw[:, :, 1], gap_e[:], gap_s[:], ALU.mult).then_inc(s_dve, 1)
                dve.wait_ge(s_dve, n.add(2))
                dve.wait_ge(s_teld, 32)
                dve.tensor_scalar(pick_all[:], expert_all[:], lane32[:], None, ALU.is_equal).then_inc(s_pick, 1)

            @block.scalar
            def _(act):
                act.wait_ge(s_gap, 1)
                act.activation(gap_e[:], gap[:], ACT.Exp).then_inc(s_gape, 1)
                act.wait_ge(s_slot, 1)

                def stage(r):
                    for h, (k0, m) in enumerate(HALVES):
                        if looped(r):
                            act.wait_ge(s_disp[h], r * (16 * TOPK * m))
                        act.activation(disp_rows[:, k0:k0 + m, :].rearrange("p s d -> p (s d)"),
                                       xh[:, ds(r * (GT * D) + k0 * D, m * D)], ACT.Copy).then_inc(s_pst[h], 1)
                        act.activation(pair_idx[h][:], slot[:, ds(r * (GT * TOPK) + k0 * TOPK, m * TOPK)],
                                       ACT.Copy).then_inc(s_pst[h], 1)

                stage(0)
                with act.Fori(1, NG) as r:
                    stage(r)

            @block.gpsimd
            def _(pool):
                with pool.Fori(0, NG) as r:
                    for h, (k0, m) in enumerate(HALVES):
                        pool.wait_ge(s_pst[h], r * 2 + 2)
                        pool.sem_inc(s_apart, 1)
                        for i in range(m):
                            for k in range(TOPK):
                                c = i * TOPK + k
                                pool.indirect_dma_start(disp_dram, bass.IndirectOffsetOnAxis(pair_idx[h][:, c:c + 1], 0),
                                                        disp_rows[:, k0 + i, :], None).then_inc(s_disp[h], 16)
                for h, (_, m) in enumerate(HALVES):
                    pool.wait_ge(s_disp[h], 16 * TOPK * m * NG)

        s_tok = [sem(f"rows_loaded{i}") for i in range(2)]
        s_tT = sem("rows_transposed")
        s_tTe = sem("rows_transpose_copied")
        s_pk = sem("bias_pick")
        s_h = sem("expert_hidden_sums")
        s_hr = sem("expert_hidden")
        s_hidT = sem("expert_hidden_transposed")
        s_hidTe = sem("expert_hidden_transpose_copied")
        s_y = sem("expert_sums")
        s_yr = sem("expert_rows")
        s_yst = [sem(f"expert_rows_stored{i}") for i in range(2)]
        assert XT % 2 == 0
        E_STEPS = (-2, XT, 2, (XT - 2) // 2)

        def is_tile(t):
            return looped(t) or 0 <= t < XT

        with nc.Block() as block:
            @block.sync
            def _(sp):
                def step(j, k):
                    t, p, half = tile_at(j, k + 2)
                    if is_tile(t):
                        if over(t - 1):
                            sp.wait_ge(s_tT, t - 1)
                        sp.dma_start(tok[p], disp_dram[ds(t * P, P), :]).then_inc(s_tok[p], 16)
                    t, p, half = tile_at(j, k - 1)
                    if is_tile(t):
                        sp.wait_ge(s_yr, t + 1)
                        sp.dma_start(expout_dram[ds(t * P, P), :], yrow[p]).then_inc(s_yst[p], 16)

                run_steps(sp, step, *E_STEPS)
                for p in range(2):
                    sp.wait_ge(s_yst[p], 16 * (XT // 2))

            @block.tensor
            def _(pe):
                pe.wait_ge(s_w1, 16)
                pe.wait_ge(s_w2, 16)
                pe.wait_ge(s_teld, 32)

                def expert(t):
                    return pe.value_load(expert_row[0:1, ds(t, 1)], min_val=0, max_val=NX - 1)

                def step(j, k):
                    t, p, _ = tile_at(j, k)
                    if is_tile(t):
                        e = expert(t)
                        pe.wait_ge(s_tTe, t + 1)
                        pe.wait_ge(s_pk, t + 1)
                        if over(t - 1):
                            pe.wait_ge(s_hr, t - 1)
                        pe.matmul(bank[2 + p][:], pick[p], bias_split[:, 0:F], start=True, stop=False)
                        for c in range(DC):
                            mm = pe.matmul(bank[2 + p][:], tokT[p][:, c * P:(c + 1) * P],
                                           lower[:, ds(e * (DC * F) + c * F, F)], start=False, stop=c == DC - 1)
                        mm.then_inc(s_h, 1)
                    t, p, _ = tile_at(j, k - 1)
                    if is_tile(t):
                        e = expert(t)
                        pe.wait_ge(s_hidTe, t + 1)
                        if over(t - 1):
                            pe.wait_ge(s_yr, t - 1)
                        pe.matmul(bank[6 + p][:, 0:D], pick[p], bias_split[:, F:F + D], start=True, stop=False)
                        for m in range(FC):
                            mm = pe.matmul(bank[6 + p][:, 0:D], hidT[p][:, m * P:(m + 1) * P],
                                           upper[:, ds(e * (FC * D) + m * D, D)], start=False, stop=m == FC - 1)
                        mm.then_inc(s_y, 1)
                    t, p, _ = tile_at(j, k)
                    if is_tile(t):
                        pe.wait_ge(s_hr, t + 1)
                        if over(t - 1):
                            pe.wait_ge(s_hidTe, t - 1)
                        for m in range(FC):
                            mm = pe.transpose(bank[4 + p][:, m * P:(m + 1) * P], hid[p][:, m * P:(m + 1) * P], ident[:])
                        mm.then_inc(s_hidT, 1)
                    t, p, half = tile_at(j, k + 2)
                    if is_tile(t):
                        pe.wait_ge(s_tok[p], half * 16 + 16)
                        if over(t):
                            pe.wait_ge(s_tTe, t)
                        for c in range(DC):
                            mm = pe.transpose(bank[p][:, c * P:(c + 1) * P], tok[p][:, c * P:(c + 1) * P], ident[:])
                        mm.then_inc(s_tT, 1)

                run_steps(pe, step, *E_STEPS)

            @block.scalar
            def _(act):
                def step(j, k):
                    t, p, _ = tile_at(j, k)
                    if is_tile(t):
                        act.wait_ge(s_hidT, t + 1)
                        if over(t - 1):
                            act.wait_ge(s_y, t - 1)
                        act.activation(hidT[p], bank[4 + p][:], ACT.Copy).then_inc(s_hidTe, 1)
                    t, p, _ = tile_at(j, k + 2)
                    if is_tile(t):
                        act.wait_ge(s_tT, t + 1)
                        if over(t - 1):
                            act.wait_ge(s_h, t - 1)
                        act.activation(tokT[p], bank[p][:, 0:D], ACT.Copy).then_inc(s_tTe, 1)

                run_steps(act, step, *E_STEPS)

            @block.vector
            def _(dve):
                dve.wait_ge(s_pick, 1)

                def step(j, k):
                    t, p, _ = tile_at(j, k + 1)
                    if is_tile(t):
                        if over(t - 1):
                            dve.wait_ge(s_y, t - 1)
                        dve.tensor_scalar(pick[p], ones_b[:], pick_all[:, ds(t, 1)], None, ALU.mult).then_inc(s_pk, 1)
                    t, p, _ = tile_at(j, k)
                    if is_tile(t):
                        dve.wait_ge(s_h, t + 1)
                        if over(t - 1):
                            dve.wait_ge(s_hidT, t - 1)
                        dve.tensor_scalar(hid[p], bank[2 + p][:], 0.0, None, ALU.max).then_inc(s_hr, 1)
                    t, p, half = tile_at(j, k - 1)
                    if is_tile(t):
                        dve.wait_ge(s_y, t + 1)
                        if over(half):
                            dve.wait_ge(s_yst[p], half * 16)
                        dve.tensor_copy(yrow[p], bank[6 + p][:, 0:D]).then_inc(s_yr, 1)

                run_steps(dve, step, *E_STEPS)

        s_fst = [sem(f"gather_back_staged{h}") for h in range(2)]
        s_frow = [sem(f"expert_rows_landed{h}") for h in range(2)]
        s_fx2 = [sem(f"x2_loaded{h}") for h in range(2)]
        s_fmix = [sem(f"rows_mixed{h}") for h in range(2)]
        s_fvar = [sem(f"ln3_var{h}") for h in range(2)]
        s_fstd = [sem(f"ln3_std{h}") for h in range(2)]
        s_fnorm = [sem(f"rows_normed{h}") for h in range(2)]
        s_fout = [sem(f"rows_out{h}") for h in range(2)]
        s_fost = [sem(f"rows_out_stored{h}") for h in range(2)]

        with nc.Block() as block:
            @block.scalar
            def _(act):
                def rounds(r):
                    for h, (k0, m) in enumerate(HALVES):
                        if looped(r):
                            act.wait_ge(s_fmix[h], r * m)
                        act.activation(pair_idx[h][:], slot[:, ds(r * (GT * TOPK) + k0 * TOPK, m * TOPK)],
                                       ACT.Copy).then_inc(s_fst[h], 1)
                    for h, (k0, m) in enumerate(HALVES):
                        act.wait_ge(s_fvar[h], r * m + m)
                        act.activation(std[:, k0:k0 + m], mv[:, k0:k0 + m, 1], ACT.Sqrt, bias=eps_col[:]).then_inc(s_fstd[h], 1)

                rounds(0)
                with act.Fori(1, NG) as r:
                    rounds(r)

            @block.gpsimd
            def _(pool):
                with pool.Fori(0, NG) as r:
                    for h, (k0, m) in enumerate(HALVES):
                        pool.wait_ge(s_fst[h], r + 1)
                        pool.sem_inc(s_apart, 1)
                        for c in range(m * TOPK):
                            pool.indirect_dma_start(exp_rows[:, k0 * TOPK + c, :], None, expout_dram,
                                                    bass.IndirectOffsetOnAxis(pair_idx[h][:, c:c + 1], 0)
                                                    ).then_inc(s_frow[h], 16)

            @block.sync
            def _(sp):
                def load(r, h):
                    k0, m = HALVES[h]
                    if looped(r) or r >= 1:
                        sp.wait_ge(s_fout[h], r)
                    sp.dma_start(x2b_in[:, k0:k0 + m, :].rearrange("p s d -> p (s d)"),
                                 x2b_dram[:, ds(r * (GT * D) + k0 * D, m * D)]).then_inc(s_fx2[h], 16)

                def store(r, h):
                    k0, m = HALVES[h]
                    sp.wait_ge(s_fout[h], r + 1)
                    whole = m if looped(r) or r * GT + k0 + m < NT else m - 1
                    sp.dma_start(out[ds(r * (GT * P) + k0 * P, whole * P), :].rearrange("(t p) d -> p t d", p=P),
                                 out_rows[:, k0:k0 + whole, :]).then_inc(s_fost[h], 16)
                    if whole < m:
                        sp.dma_start(out[(NT - 1) * P:N, :], out_rows[0:TAIL, k0 + whole, :]).then_inc(s_fost[h], 16)

                load(0, 0)
                load(0, 1)
                with sp.Fori(1, NG) as r:
                    for h in range(2):
                        store(r - 1, h)
                        load(r, h)
                store(NG - 1, 0)
                store(NG - 1, 1)
                sp.wait_ge(s_fost[0], 16 * NG)
                sp.wait_ge(s_fost[1], 16 * (NG + 1))

            @block.vector
            def _(dve):
                n = dve_n

                def half(r, h):
                    k0, m = HALVES[h]
                    dve.wait_ge(s_frow[h], r * (16 * TOPK * m) + 16 * TOPK * m)
                    for k in range(m):
                        dve.scalar_tensor_tensor(mixed[:, k0 + k, :], exp_rows[:, (k0 + k) * TOPK, :],
                                                 mix_w[:, ds(r * (GT * TOPK) + (k0 + k) * TOPK, 1)],
                                                 xh[:, ds(r * (GT * D) + (k0 + k) * D, D)], ALU.mult, ALU.add).then_inc(s_dve, 1)
                    n.add(m)
                    for k in range(m):
                        dve.wait_ge(s_dve, n.back(m - 1 - k))
                        dve.scalar_tensor_tensor(mixed[:, k0 + k, :], exp_rows[:, (k0 + k) * TOPK + 1, :],
                                                 mix_w[:, ds(r * (GT * TOPK) + (k0 + k) * TOPK + 1, 1)],
                                                 mixed[:, k0 + k, :], ALU.mult, ALU.add).then_inc(s_fmix[h], 1)
                    for k in range(m):
                        dve.wait_ge(s_fmix[h], r * m + k + 1)
                        dve.bn_stats(stats[:, k0 + k, :], mixed[:, k0 + k, :]).then_inc(s_dve, 1)
                    n.add(m)
                    for k in range(m):
                        dve.wait_ge(s_dve, n.back(m - 1 - k))
                        dve.sem_inc(s_apart, 1)
                        dve.bn_aggr(mv[:, k0 + k, :], stats[:, k0 + k, :]).then_inc(s_fvar[h], 1)

                def finish(r, h):
                    k0, m = HALVES[h]
                    dve.wait_ge(s_fstd[h], r + 1)
                    dve.reciprocal(rstd[:, k0:k0 + m], std[:, k0:k0 + m]).then_inc(s_dve, 1)
                    dve.wait_ge(s_dve, n.add())
                    for k in range(k0, k0 + m):
                        dve.tensor_scalar(normed[:, k, :], mixed[:, k, :], mv[:, k, 0:1], rstd[:, k:k + 1],
                                          ALU.subtract, ALU.mult).then_inc(s_dve, 1)
                    dve.wait_ge(s_dve, n.add(m))
                    nv, ov = normed[:, k0:k0 + m, :], out_rows[:, k0:k0 + m, :]
                    dve.tensor_tensor(nv, nv, gamma_row[:].unsqueeze(1).to_broadcast([P, m, D]), ALU.mult).then_inc(s_dve, 1)
                    dve.wait_ge(s_dve, n.add())
                    dve.wait_ge(s_fx2[h], r * 16 + 16)
                    if looped(r) or r >= 1:
                        dve.wait_ge(s_fost[h], r * 16)
                    dve.tensor_tensor(ov, nv, x2b_in[:, k0:k0 + m, :], ALU.add).then_inc(s_fout[h], 1)
                    dve.wait_ge(s_fout[h], r + 1)

                def rounds(r):
                    half(r, 0)
                    half(r, 1)
                    finish(r, 0)
                    finish(r, 1)

                at0 = n.n
                rounds(0)
                per_round = n.n - at0
                with dve.Fori(1, NG) as r:
                    n.enter(r - 1, per_round)
                    rounds(r)
                    n.leave(NG - 1)


_INS = ["x", "src", "dst", "edge_weight", "L0_gnn_W1", "L0_gnn_b1", "L0_gnn_W2", "L0_gnn_b2",
        "L0_mix_kln_weight", "L0_mix_kln_bias", "L0_mix_vln_weight", "L0_mix_vln_bias",
        "L0_ffn_gate_w", "L0_ffn_gate_b", "L0_ffn_w1", "L0_ffn_b1", "L0_ffn_w2", "L0_ffn_b2",
        "L0_ffn_gamma", "L0_ffn_beta"]


def kernel(**inputs):
    import numpy as _np
    import concourse.bacc as _bacc
    from concourse import mybir as _mybir
    from concourse.bass_utils import run_bass_kernel_spmd as _run

    nc = _bacc.Bacc("TRN2", target_bir_lowering=False, num_devices=1)
    arrays, args = {}, []
    for name in _INS:
        a = _np.ascontiguousarray(inputs[name])
        arrays[f"in_{name}"] = a
        args.append(nc.dram_tensor(f"in_{name}", a.shape, _mybir.dt.from_np(a.dtype), kind="ExternalInput").ap())
    out = nc.dram_tensor("out_rows_dram", inputs["x"].shape, _mybir.dt.float32, kind="ExternalOutput").ap()
    gps_layer(nc, *args, out)
    r = _run(nc, [arrays], core_ids=[0])
    return r.results[0]["out_rows_dram"]
```

```python
from contextlib import ExitStack

import concourse.bass as bass
from concourse import mybir

F32 = mybir.dt.float32
I32 = mybir.dt.int32
U32 = mybir.dt.uint32
U16 = mybir.dt.uint16
BF16 = mybir.dt.bfloat16
ALU = mybir.AluOpType
ACT = mybir.ActivationFunctionType
AX = mybir.AxisListType.X
ds = bass.ds

P = 128
LN_EPS = 1e-5
HEADS = 8


class Steps:

    def __init__(self):
        self.n = 0
        self.shift = 0

    def add(self, k=1):
        self.n += k
        return self.shift + self.n

    def back(self, k):
        return self.shift + (self.n - k)

    def enter(self, rounds_done, per_round):
        self.shift = rounds_done * per_round
        self.at, self.per = self.n, per_round

    def leave(self, rounds):
        assert self.n - self.at == self.per, (self.n - self.at, self.per)
        self.n = self.at + rounds * self.per
        self.shift = 0


def gps_layer(nc, x, src, dst, edge_weight, gW1, gb1, gW2, gb2, klw, klb, vlw, vlb,
              gate_w, gate_b, w1, b1, w2, b2, gamma, beta, out):
    N, D = x.shape
    E = src.shape[0]
    H = gW1.shape[1]
    NX, _, F = w1.shape
    HD = D // HEADS
    DC = D // P
    HC = H // P
    FC = F // P
    TOPK = 2
    NT = -(-N // P)
    TAIL = N - (NT - 1) * P
    GT = 7
    NG = NT // GT
    assert NG * GT == NT and NT % 2 == 1

    CH, SC, QB = 7, 112, 7
    NBUF = 4
    EC = CH * SC
    assert P * EC >= E > (P - 1) * EC and SC % (NBUF * QB) == 0
    EFULL = E // EC
    EREST = E - EFULL * EC
    GB, GBUF = 8, 4
    ROUND = GB * GBUF
    ET = -(-((P * EC + NT * (P - 1)) // P) // ROUND) * ROUND
    EROUNDS = ET // ROUND
    REC = 4
    BT = -(-ET // P)
    XT = (TOPK * NT * P + NX * (P - 1)) // P
    XT += (XT % 2)
    NJ = TOPK * NT
    NTP = NT * P
    NBLK = 8 * P
    assert XT <= P and NX * NT + P <= NBLK

    rec_dram = nc.dram_tensor("edge_records_sorted", [P, ET * REC], F32).ap()
    xn_dram = nc.dram_tensor("xn_rows", [NT * P, D], F32).ap()
    x2b_dram = nc.dram_tensor("x2_plus_beta", [P, NT * D], F32).ap()
    bucket_dram = nc.dram_tensor("bucket_of_tile", [BT * P], I32).ap()
    ids_dram = nc.dram_tensor("dispatched_ids", [NBLK, P], F32).ap()
    xn2_dram = nc.dram_tensor("xn2_rows", [NTP, D], F32).ap()
    y_dram = nc.dram_tensor("expert_rows", [TOPK * NTP + XT * P, D], F32).ap()

    ctx = ExitStack()
    with ctx:
        def sb(name, shape, dt=F32):
            return ctx.enter_context(nc.sbuf_tensor(name, shape, dt))

        def sem(name):
            return ctx.enter_context(nc.semaphore(name))

        bank = [ctx.enter_context(nc.psum_tensor(f"bank{i}", [P, 512], F32)) for i in range(8)]

        xh = sb("xh", [P, NT * D])
        upper = sb("upper", [P, NX * FC * D])
        res = upper[:, 0:NT * D]
        spare = upper[:, NT * D:NX * FC * D]
        lower = sb("lower", [P, NX * DC * F])
        AW = 8 * D + 2 * F + 2 * DC * F + P
        arena = sb("arena", [P, AW])

        def carver(region, size):
            at = [0]

            def carve(words):
                a = at[0]
                at[0] += words
                assert at[0] <= size, (at[0], size)
                return region[:, a:a + words]
            return carve

        w1_sb = lower[:, :].rearrange("p (e c f) -> p e c f", e=NX, c=DC)
        w2_sb = upper[:, :].rearrange("p (e m d) -> p e m d", e=NX, m=FC)

        carve = carver(lower, NX * DC * F)
        records = carve(EC * REC).rearrange("p (j c) -> p j c", c=REC)
        src_i = carve(EC).bitcast(I32)
        dst_i = carve(EC).bitcast(I32)
        wgt = carve(EC)
        bkt_i = carve(EC).bitcast(I32)
        bkt_f = carve(EC // 2).bitcast(BF16)
        match = [carve(EC // 2).bitcast(BF16) for _ in range(2)]
        masks = [carve(SC // 2).bitcast(U16) for _ in range(4)]
        cums = carve(NT * SC).rearrange("p (b j) -> p b j", b=NT)
        rank = carve(SC)
        slot_i = carve(SC).bitcast(I32)
        tile_i = carve(SC).bitcast(I32)
        row_i = carve(SC).bitcast(I32)
        sq = carve(GT * D)
        kvt = carve(DC * P).rearrange("p (c e) -> p c e", c=DC)
        kvs = carve(DC * P).rearrange("p (c e) -> p c e", c=DC)
        past = carve(BT * NT).rearrange("p (c b) -> p c b", c=BT)
        carve = carver(lower, NX * DC * F)
        sorted_rec = carve(ET * REC).rearrange("p (t c) -> p t c", c=REC)
        edge_rows = carve(ROUND * D).rearrange("p (s d) -> p s d", d=D)
        gath_idx = [carve(GB).bitcast(U32) for _ in range(GBUF)]
        edge_sel = carve(ROUND * P).rearrange("p (s n) -> p s n", n=P)
        carve = carver(lower, NX * DC * F)
        gamma_row = carve(D)
        exp_rows = carve(TOPK * GT * D).rearrange("p (k s d) -> p k s d", k=TOPK, d=D)
        mixed = carve(GT * D).rearrange("p (s d) -> p s d", d=D)
        normed = carve(GT * D).rearrange("p (s d) -> p s d", d=D)
        x2b_in = carve(GT * D).rearrange("p (s d) -> p s d", d=D)
        out_rows = carve(GT * D).rearrange("p (s d) -> p s d", d=D)
        carve = carver(spare, NX * FC * D - NT * D)
        zeros = carve(ET * REC)
        PADB = 2
        pads = carve(PADB * P)
        gb2_row = carve(D)
        carve = carver(spare, NX * FC * D - NT * D)
        gW1_sb = carve(DC * H).rearrange("p (c f) -> p c f", c=DC)
        gW2_sb = carve(HC * D).rearrange("p (c d) -> p c d", c=HC)
        bucket_row = carve(BT * P).bitcast(I32)[0:1, :]
        before_b = carve(P // 2).bitcast(BF16)
        ones_pb = carve(P // 2).bitcast(BF16)
        carve = carver(arena, AW)
        nd = carve(GT * D)
        kvm = carve(DC * P).rearrange("p (c e) -> p c e", c=DC)
        blockdiag = carve(P)
        vw_row = carve(D)
        vb_row = carve(D)
        xin = [carve(D) for _ in range(2)]
        xT = [carve(D) for _ in range(2)]
        scat_idx = [carve(QB).bitcast(U32) for _ in range(NBUF)]
        scat_rec = [carve(QB * REC).rearrange("p (j c) -> p j c", c=REC) for _ in range(NBUF)]
        cnt = carve(NT)
        base = carve(NT)
        hsum, hstd, hr = (carve(GT * HEADS) for _ in range(3))
        carve = carver(arena, AW)
        hin = [carve(D) for _ in range(2)]
        hT = [carve(D) for _ in range(2)]
        g1 = [carve(H) for _ in range(2)]
        x2 = [carve(D) for _ in range(2)]
        x2b = [carve(D) for _ in range(2)]
        xn2 = [carve(D) for _ in range(2)]
        xn2T = [carve(D) for _ in range(2)]
        beta_row = carve(D)
        hot = [carve(TOPK * NX).rearrange("p (k e) -> p k e", k=TOPK) for _ in range(2)]
        hot_both = [carve(NX // 2).bitcast(BF16) for _ in range(2)]
        hot_sum = [carve(NX // 2).bitcast(BF16) for _ in range(2)]
        place = carve(NX)
        hot_place = carve(TOPK * NX).rearrange("p (k e) -> p k e", k=TOPK)
        ids_all = carve(NJ)
        carve = carver(arena, AW)
        past_x = carve(NX - 1)
        past_tiles = carve(NX - 1)
        first_tile = carve(1)
        block_f = carve(1)
        block_i = carve(1).bitcast(U32)
        expert_wide = carve(96)
        ids_tile = carve(P)
        second = carve(XT)
        pad = carve(XT)
        node1 = carve(XT)
        pad_tile = carve(XT)
        gap = carve(NT)
        gap_e = carve(NT)
        gap_s = carve(NT)
        carve = carver(arena, AW)
        tok = [carve(D) for _ in range(2)]
        tokT = [carve(D) for _ in range(2)]
        w1_tile = [carve(DC * F) for _ in range(2)]
        hidT = [carve(F) for _ in range(2)]
        yrow = [carve(D) for _ in range(2)]
        pick = [carve(P // 2).bitcast(BF16)[0:96, :] for _ in range(2)]

        ident = sb("ident", [P, P])
        ones = sb("ones", [P, P])
        before = sb("before", [P, P])
        iota_n = sb("iota_n", [P, P])
        iota_pc = sb("iota_pc", [P, BT])
        eps_col = sb("eps_col", [P, 1])
        gb1_col = sb("gb1_col", [P, HC])
        kw_col = sb("kw_col", [P, DC])
        kb_col = sb("kb_col", [P, DC])
        gate_sb = sb("gate_sb", [P, DC, NX])
        gateb_row = sb("gateb_row", [P, NX])
        bias_split = sb("bias_split", [96, F + D], BF16)
        lane_i = sb("lane_i", [96, 1], I32)
        lane32 = sb("lane32", [96, 1])

        tiles_i = sb("tiles_i", [P, NT], I32)
        tiles_f = sb("tiles_f", [P, NT])
        ends = sb("ends", [P, NT])
        tile_bucket = sb("tile_bucket", [P, BT])
        tile_bucket_i = sb("tile_bucket_i", [P, BT], I32)
        stats = sb("stats", [P, GT, 6])
        mv = sb("mv", [P, GT, 2])
        std = sb("std", [P, GT])
        rstd = sb("rstd", [P, GT])
        ncol = sb("ncol", [P, DC])
        logits = sb("logits", [P, NX])
        top8 = sb("top8", [P, 8])
        idx8 = sb("idx8", [P, 8], U32)
        topv = sb("topv", [P, NJ])
        top_f = [sb(f"top_f{i}", [P, TOPK]) for i in range(2)]
        slot2 = [sb(f"slot2_{i}", [P, TOPK]) for i in range(2)]
        slot_idx = [sb(f"slot_idx{i}", [P, TOPK], U32) for i in range(2)]
        slot_id = [sb(f"slot_id{i}", [P, TOPK]) for i in range(2)]
        expert_at = sb("expert_at", [P, NX])
        mix_w = sb("mix_w", [P, NJ])
        tile_expert = sb("tile_expert", [P, 1])
        node_all = sb("node_all", [P, XT])
        dest_all = sb("dest_all", [P, XT])
        b1_tile = sb("b1_tile", [P, FC * XT])
        tok_idx = [sb(f"tok_idx{i}", [P, 1], U32) for i in range(2)]
        dest_idx = [sb(f"dest_idx{i}", [P, 1], U32) for i in range(2)]
        pick_all = sb("pick_all", [96, P], BF16)
        ones_b = sb("ones_b", [96, P], BF16)
        expert_row = sb("expert_row", [1, P], I32)
        st2 = sb("st2", [P, 6])
        mv2 = [sb(f"mv2_{i}", [P, 2]) for i in range(2)]
        std2 = [sb(f"std2_{i}", [P, 1]) for i in range(2)]
        rstd2 = sb("rstd2", [P, 1])
        HA = (GT + 1) // 2
        HALVES = ((0, HA), (HA, GT - HA))

        rows_of = lambda a, t0, n: a[t0 * P:(t0 + n) * P, :].rearrange("(t p) d -> p t d", p=P)
        dve_n = Steps()
        s_dve = sem("dve_steps")
        s_apart = sem("waits_apart")

        def row(a):
            return a.rearrange("(o d) -> o d", o=1).partition_broadcast(P).rearrange("p o d -> p (o d)")

        def looped(n):
            return not isinstance(n, int)

        def tile_ends(dve, nb, totals):
            dve.tensor_scalar(tiles_i[:, 0:nb], totals, float(P - 1), None, ALU.add).then_inc(s_dve, 1)
            dve.wait_ge(s_dve, dve_n.add())
            dve.tensor_scalar(tiles_i[:, 0:nb], tiles_i[:, 0:nb], 7, None, ALU.arith_shift_right).then_inc(s_dve, 1)
            dve.wait_ge(s_dve, dve_n.add())
            dve.tensor_copy(tiles_f[:, 0:nb], tiles_i[:, 0:nb]).then_inc(s_dve, 1)
            dve.wait_ge(s_dve, dve_n.add())
            dve.tensor_tensor_scan(ends[:, 0:nb], ones[:, 0:nb], tiles_f[:, 0:nb], 0.0, ALU.mult, ALU.add).then_inc(s_dve, 1)
            dve.wait_ge(s_dve, dve_n.add())

        s_emset = sem("edge_pads_cleared")
        s_edges = sem("edges_loaded")
        s_xtail = sem("x_tail_cleared")
        s_x = sem("x_loaded")
        s_par = sem("weights_loaded")
        s_poolc = sem("constants_begun")
        s_consts = sem("constants_made")
        s_ones = sem("ones_made")
        s_zero = sem("zeros_made")
        s_recz = sem("records_zeroed")
        s_idz = sem("dispatch_ids_filled")
        s_bias0 = sem("bias_cleared")
        s_cnt = sem("buckets_counted")
        s_pref = sem("bucket_prefix")
        s_bk = sem("tile_buckets")
        s_bkst = sem("tile_buckets_stored")
        s_bkld = sem("tile_buckets_loaded")
        s_addr = sem("edge_addresses")
        s_stage = [sem(f"scatter_staged{q}") for q in range(NBUF)]
        s_scat = [sem(f"scatter_landed{q}") for q in range(NBUF)]
        s_var = sem("ln1_var")
        s_std = sem("ln1_std")
        s_xn = sem("xn_tiles")
        s_xnst = sem("xn_stored")
        s_dev = sem("heads_centred")
        s_sq = sem("heads_squared")
        s_hss = sem("heads_sumsq")
        s_hstd = sem("heads_std")
        s_nd = sem("heads_normed")
        s_kvmm = sem("kv_products")
        s_kv = sem("kv_matrix")
        s_xin = sem("xn_staged")
        s_xT = sem("xn_transposed")
        s_xTe = sem("xn_transpose_copied")
        s_att = sem("attention_rows")
        s_res = sem("residual_rows")
        QCOLS = NBUF * QB
        QROUNDS = EC // QCOLS
        QPERCH = SC // QCOLS
        bias_f = sq[0:96, 0:F + D]
        bias_r = sq[0:96, F + D:2 * (F + D)]
        assert 2 * (F + D) <= GT * D

        with nc.Block() as block:
            @block.sync
            def _(sp):
                lo = EFULL // 16 * 16
                for n, (tile, a) in enumerate(((src_i, src), (dst_i, dst), (wgt, edge_weight))):
                    sp.wait_ge(s_emset, n + 1)
                    sp.dma_start(tile[0:lo, :], a[0:lo * EC].rearrange("(p j) -> p j", j=EC)).then_inc(s_edges, 16)
                    sp.dma_start(tile[lo:EFULL, :],
                                 a[lo * EC:EFULL * EC].rearrange("(p j) -> p j", j=EC)).then_inc(s_edges, 16)
                    sp.dma_start(tile[EFULL:EFULL + 1, 0:EREST],
                                 a[EFULL * EC:E].rearrange("(p j) -> p j", p=1)).then_inc(s_edges, 16)
                sp.wait_ge(s_zero, 1)
                sp.dma_start(rec_dram, zeros[:, 0:ET * REC]).then_inc(s_recz, 16)
                xv = res.rearrange("p (t d) -> p t d", d=D)
                sp.dma_start(xv[:, 0:NT - 1, :], rows_of(x, 0, NT - 1)).then_inc(s_x, 16)
                sp.wait_ge(s_xtail, 1)
                sp.dma_start(xv[0:TAIL, NT - 1, :], x[(NT - 1) * P:N, :]).then_inc(s_x, 16)

                def flat(a):
                    return a.rearrange("h o d -> (h o d)")

                for to, a in ((gate_sb[:], gate_w.rearrange("(c p) e -> p c e", p=P)),
                              (gb2_row, row(gb2)), (vw_row, row(flat(vlw))), (vb_row, row(flat(vlb))),
                              (gateb_row[:], row(gate_b))):
                    sp.dma_start(to, a).then_inc(s_par, 16)
                with nc.allow_non_contiguous_dma(reason="short columns of weights"):
                    for to, a in ((gb1_col, gb1), (kw_col, flat(klw)), (kb_col, flat(klb))):
                        sp.dma_start(to[:], a.rearrange("(c p) -> p c", p=P)).then_inc(s_par, 16)
                sp.wait_ge(s_bias0, 1)
                for q in range(3):
                    sp.dma_start(bias_f[32 * q:32 * q + NX, 0:F], b1).then_inc(s_par, 16)
                    sp.dma_start(bias_f[32 * q:32 * q + NX, F:F + D], b2).then_inc(s_par, 16)
                sp.wait_ge(s_consts, 8)
                fill = ids_dram.rearrange("(h p b) l -> h p (b l)", p=P, b=PADB)
                for k in range(NBLK // (P * PADB)):
                    sp.dma_start(fill[k], pads).then_inc(s_idz, 16)
                sp.wait_ge(s_bk, 1)
                with nc.allow_non_contiguous_dma(reason="a column to a row"):
                    sp.dma_start(bucket_dram.rearrange("(c p) -> p c", p=P), tile_bucket_i[:]).then_inc(s_bkst, 16)
                with sp.Fori(0, NG) as g:
                    sp.wait_ge(s_xn, g * GT + GT)
                    sp.dma_start(xn_dram[ds(g * (GT * P), GT * P), :].rearrange("(t p) d -> p t d", p=P),
                                 xh[:, ds(g * (GT * D), GT * D)].rearrange("p (t d) -> p t d", d=D)).then_inc(s_xnst, 16)
                sp.wait_ge(s_xnst, 16 * NG)
                sp.wait_ge(s_idz, 16 * (NBLK // (P * PADB)))
                sp.wait_ge(s_bkst, 16)

            @block.gpsimd
            def _(pool):
                pool.memset(ident[:], 0.0).then_inc(s_poolc, 1)
                pool.memset(before[:], 1.0).then_inc(s_poolc, 1)
                pool.iota(iota_n[:], pattern=[[1, P]], base=0, channel_multiplier=0,
                          allow_small_or_imprecise_dtypes=True).then_inc(s_consts, 1)
                pool.iota(iota_pc[:], pattern=[[P, BT]], base=0, channel_multiplier=1,
                          allow_small_or_imprecise_dtypes=True).then_inc(s_consts, 1)
                pool.iota(lane_i[:], pattern=[[0, 1]], base=0, channel_multiplier=1).then_inc(s_consts, 1)
                pool.wait_ge(s_poolc, 2)
                pool.affine_select(out=ident[:], in_=ident[:], compare_op=ALU.not_equal, fill=1.0, base=0,
                                   pattern=[[-1, P]], channel_multiplier=1).then_inc(s_consts, 1)
                pool.affine_select(out=before[:], in_=before[:], compare_op=ALU.is_gt, fill=0.0, base=0,
                                   pattern=[[1, P]], channel_multiplier=-1).then_inc(s_consts, 1)

                def stage(r, q):
                    pool.tensor_copy(scat_idx[q], records[:, ds(r * QCOLS + q * QB, QB), 3]).then_inc(s_stage[q], 1)
                    pool.tensor_copy(scat_rec[q], records[:, ds(r * QCOLS + q * QB, QB), :]).then_inc(s_stage[q], 1)

                def send(r, q):
                    pool.wait_ge(s_stage[q], r * 2 + 2)
                    pool.sem_inc(s_apart, 1)
                    for c in range(QB):
                        pool.indirect_dma_start(rec_dram.rearrange("p (t c) -> (p t) c", c=REC),
                                                bass.IndirectOffsetOnAxis(scat_idx[q][:, c:c + 1], 0),
                                                scat_rec[q][:, c, :], None).then_inc(s_scat[q], 16)

                pool.iota(ids_all, pattern=[[P, NT], [NTP, TOPK]], base=0, channel_multiplier=1,
                          allow_small_or_imprecise_dtypes=True).then_inc(s_consts, 1)
                pool.iota(expert_at[:], pattern=[[NTP, NX]], base=0, channel_multiplier=0,
                          allow_small_or_imprecise_dtypes=True).then_inc(s_consts, 1)
                pool.iota(pads, pattern=[[0, PADB], [1, P]], base=TOPK * NTP, channel_multiplier=0,
                          allow_small_or_imprecise_dtypes=True).then_inc(s_consts, 1)
                pool.wait_ge(s_recz, 16)
                pool.wait_ge(s_addr, 1)
                stage(0, 0)
                for q in range(NBUF):
                    if q + 1 < NBUF:
                        stage(0, q + 1)
                    else:
                        pool.wait_ge(s_scat[0], 16 * QB)
                        stage(1, 0)
                    send(0, q)
                with pool.Fori(1, QROUNDS - 1) as r:
                    pool.wait_ge(s_addr, r + 2)
                    for q in range(NBUF):
                        n, rn = (q + 1, r) if q + 1 < NBUF else (0, r + 1)
                        pool.wait_ge(s_scat[n], rn * (16 * QB))
                        stage(rn, n)
                        send(r, q)
                for q in range(NBUF):
                    if q + 1 < NBUF:
                        pool.wait_ge(s_scat[q + 1], 16 * QB * (QROUNDS - 1))
                        stage(QROUNDS - 1, q + 1)
                    send(QROUNDS - 1, q)
                for q in range(NBUF):
                    pool.wait_ge(s_scat[q], 16 * QB * QROUNDS)

            @block.tensor
            def _(pe):
                pe.wait_ge(s_ones, 1)
                pe.wait_ge(s_consts, 5)
                pe.wait_ge(s_cnt, NT)
                pe.matmul(bank[0][:, 0:NT], ones[:], cnt, start=True, stop=True).then_inc(s_pref, 1)
                pe.matmul(bank[1][:, 0:NT], before[:], cnt, start=True, stop=True).then_inc(s_pref, 1)

                def sums(g):
                    pe.wait_ge(s_nd, g + 1)
                    for k in range(GT):
                        first = not looped(g) and g == 0 and k == 0
                        last = not looped(g) and g == NG - 1 and k == GT - 1
                        for c in range(DC):
                            a = nd[:, k * D + c * P:k * D + (c + 1) * P]
                            pe.matmul(bank[2 + c][:, 0:P], a, a, start=first, stop=last)
                            pe.matmul(bank[4 + c][:, 0:1], a, ones[:, 0:1], start=first, stop=last)
                        mm = pe.matmul(bank[6][:, 0:D], ones[:], nd[:, k * D:(k + 1) * D], start=first, stop=last)
                    mm.then_inc(s_kvmm, 1)

                sums(0)
                with pe.Fori(1, NG - 1) as g:
                    sums(g)
                sums(NG - 1)

                def turn(t, p):
                    pe.wait_ge(s_xin, t + 1)
                    for c in range(DC):
                        mm = pe.transpose(bank[p][:, c * P:(c + 1) * P], xin[p][:, c * P:(c + 1) * P], ident[:])
                    mm.then_inc(s_xT, 1)

                def attend(t, p):
                    pe.wait_ge(s_xTe, t + 1)
                    for c in range(DC):
                        mm = pe.matmul(bank[2 + p][:, c * P:(c + 1) * P], xT[p][:, c * P:(c + 1) * P], kvm[:, c, :],
                                       start=True, stop=True)
                    mm.then_inc(s_att, 1)

                def step(t, p):
                    turn(t, p)
                    if looped(t) or t >= 1:
                        if looped(t) or t >= 3:
                            pe.wait_ge(s_res, t - 2)
                        attend(t - 1, 1 - p)

                pe.wait_ge(s_kv, 1)
                for t in range(3):
                    step(t, t % 2)
                with pe.Fori(0, (NT - 3) // 2) as j:
                    step(j * 2 + 3, 1)
                    step(j * 2 + 4, 0)
                pe.wait_ge(s_res, NT - 2)
                attend(NT - 1, (NT - 1) % 2)

            @block.scalar
            def _(act):
                with act.Fori(0, NG) as g:
                    act.wait_ge(s_var, g * GT + GT)
                    act.activation(std[:], mv[:, :, 1], ACT.Sqrt, bias=eps_col[:]).then_inc(s_std, 1)
                with act.Fori(0, NG) as g:
                    act.wait_ge(s_dev, g + 1)
                    act.activation(sq, nd, ACT.Square).then_inc(s_sq, 1)
                    act.wait_ge(s_hss, g + 1)
                    act.activation(hstd, hsum, ACT.Sqrt, scale=1.0 / (HD - 1)).then_inc(s_hstd, 1)

                def step(t, p):
                    if looped(t) or t < NT:
                        if looped(t) or t >= 2:
                            act.wait_ge(s_xT, t - 1)
                        act.activation(xin[p], xh[:, ds(t * D, D)], ACT.Copy).then_inc(s_xin, 1)
                    if looped(t) or t >= 1:
                        act.wait_ge(s_xT, t)
                        if looped(t) or t >= 3:
                            act.wait_ge(s_att, t - 2)
                        act.activation(xT[1 - p], bank[1 - p][:, 0:D], ACT.Copy).then_inc(s_xTe, 1)

                act.wait_ge(s_kv, 1)
                for t in range(3):
                    step(t, t % 2)
                with act.Fori(0, (NT - 3) // 2) as j:
                    step(j * 2 + 3, 1)
                    step(j * 2 + 4, 0)
                step(NT, NT % 2)

            @block.vector
            def _(dve):
                n = dve_n
                dve.memset(src_i, 0).then_inc(s_emset, 1)
                dve.memset(dst_i, 0).then_inc(s_emset, 1)
                dve.memset(wgt, 0.0).then_inc(s_emset, 1)
                dve.memset(zeros, 0.0).then_inc(s_zero, 1)
                dve.memset(ones[:], 1.0).then_inc(s_ones, 1)
                dve.memset(res[:, (NT - 1) * D:NT * D], 0.0).then_inc(s_xtail, 1)
                dve.memset(bias_f, 0.0).then_inc(s_bias0, 1)
                dve.memset(eps_col[:], LN_EPS).then_inc(s_dve, 1)
                dve.memset(ones_b[:], 1.0).then_inc(s_dve, 1)
                dve.memset(blockdiag, 0.0).then_inc(s_dve, 1)
                dve.wait_ge(s_dve, n.add(3))
                for q in range(P // HD):
                    dve.memset(blockdiag[q * HD:(q + 1) * HD, q * HD:(q + 1) * HD], 1.0 / N).then_inc(s_dve, 1)
                dve.wait_ge(s_edges, 16 * 9)
                dve.tensor_scalar(bkt_i, src_i, 7, None, ALU.arith_shift_right).then_inc(s_dve, 1)
                dve.wait_ge(s_dve, n.add(P // HD + 1))
                dve.tensor_copy(bkt_f, bkt_i).then_inc(s_dve, 1)
                dve.wait_ge(s_dve, n.add())
                dve.wait_ge(s_consts, 5)
                with dve.Fori(0, NT // GT) as r:
                    for k in range(GT):
                        if k >= 2:
                            dve.wait_ge(s_cnt, r * GT + k - 1)
                        dve.tensor_scalar(match[k % 2], bkt_f, iota_n[:, ds(r * GT + k, 1)], 0.0, ALU.is_equal, ALU.add,
                                          accum_out=cnt[:, ds(r * GT + k, 1)]).then_inc(s_cnt, 1)
                    dve.wait_ge(s_cnt, r * GT + GT)
                dve.tensor_copy(records[:, :, 0], dst_i).then_inc(s_dve, 1)
                dve.tensor_scalar(bkt_i, src_i, P - 1, None, ALU.bitwise_and).then_inc(s_dve, 1)
                dve.tensor_copy(records[:, :, 2], wgt).then_inc(s_dve, 1)
                dve.wait_ge(s_dve, n.add(3))
                dve.tensor_copy(records[:, :, 1], bkt_i).then_inc(s_dve, 1)
                dve.wait_ge(s_dve, n.add())
                dve.wait_ge(s_pref, 2)
                tile_ends(dve, NT, bank[0][:, 0:NT])
                dve.tensor_tensor(base, ends[:], tiles_f[:], ALU.subtract).then_inc(s_dve, 1)
                dve.wait_ge(s_dve, n.add())
                dve.scalar_tensor_tensor(base, base, float(P), bank[1][:, 0:NT], ALU.mult, ALU.add).then_inc(s_dve, 1)
                dve.wait_ge(s_dve, n.add())
                dve.tensor_copy(cums[:, :, SC - 1], base).then_inc(s_dve, 1)
                dve.wait_ge(s_dve, n.add())

                per_chunk = 3 * NT + 4
                with dve.Fori(0, CH) as ch:
                    n.enter(ch, per_chunk)
                    for b in range(NT + 2):
                        if b < NT:
                            dve.wait_ge(s_dve, n.back(2))
                            dve.tensor_scalar(masks[b % 4], bkt_f[:, ds(ch * SC, SC)], float(b), None,
                                              ALU.is_equal).then_inc(s_dve, 1)
                            n.add()
                        if 1 <= b <= NT:
                            dve.wait_ge(s_dve, n.back(1 if b < NT else 0))
                            dve.tensor_tensor_scan(cums[:, b - 1, :], ones[:, 0:SC], masks[(b - 1) % 4],
                                                   cums[:, b - 1, SC - 1:SC], ALU.mult, ALU.add).then_inc(s_dve, 1)
                            n.add()
                        if b >= 2:
                            if b > NT:
                                dve.wait_ge(s_dve, n.back(0))
                                dve.sem_inc(s_apart, 1)
                            dve.copy_predicated(rank, masks[(b - 2) % 4], cums[:, b - 2, :]).then_inc(s_dve, 1)
                            n.add()
                    dve.wait_ge(s_dve, n.back(0))
                    dve.tensor_scalar(slot_i, rank, -1.0, None, ALU.add).then_inc(s_dve, 1)
                    dve.wait_ge(s_dve, n.add())
                    dve.tensor_scalar(tile_i, slot_i, 7, None, ALU.arith_shift_right).then_inc(s_dve, 1)
                    dve.tensor_scalar(row_i, slot_i, P - 1, None, ALU.bitwise_and).then_inc(s_dve, 1)
                    dve.wait_ge(s_dve, n.add(2))
                    dve.scalar_tensor_tensor(rank, row_i, float(ET), tile_i, ALU.mult, ALU.add).then_inc(s_dve, 1)
                    dve.wait_ge(s_dve, n.add())
                    dve.tensor_copy(records[:, ds(ch * SC, SC), 3], rank).then_inc(s_addr, QPERCH)
                    dve.wait_ge(s_addr, ch * QPERCH + QPERCH)
                    n.leave(CH)

                dve.tensor_tensor(past, iota_pc[:].unsqueeze(2).to_broadcast([P, BT, NT]),
                                  ends[:].unsqueeze(1).to_broadcast([P, BT, NT]), ALU.is_ge).then_inc(s_dve, 1)
                dve.wait_ge(s_dve, n.add())
                dve.tensor_reduce(tile_bucket[:], past, AX, ALU.add).then_inc(s_dve, 1)
                dve.wait_ge(s_dve, n.add())
                dve.tensor_scalar(tile_bucket_i[:], tile_bucket[:], float(NT - 1), None, ALU.min).then_inc(s_bk, 1)

                dve.wait_ge(s_par, 16 * (5 + 3 + 6))
                thirds = [slice(32 * q, 32 * q + 32) for q in range(3)]
                for q in range(3):
                    for rows in thirds[q:]:
                        dve.tensor_copy(bias_split[rows, :], bias_f[rows, :]).then_inc(s_dve, 1)
                    dve.wait_ge(s_dve, n.add(3 - q))
                    if q < 2:
                        for rows in thirds[q + 1:]:
                            dve.tensor_copy(bias_r[rows, :], bias_split[rows, :]).then_inc(s_dve, 1)
                        dve.wait_ge(s_dve, n.add(2 - q))
                        for rows in thirds[q + 1:]:
                            dve.tensor_tensor(bias_f[rows, :], bias_f[rows, :], bias_r[rows, :],
                                              ALU.subtract).then_inc(s_dve, 1)
                        dve.wait_ge(s_dve, n.add(2 - q))

                dve.wait_ge(s_x, 32)
                with dve.Fori(0, NG) as g:
                    n.enter(g, GT + 1)
                    for k in range(GT):
                        dve.bn_stats(stats[:, k, :], res[:, ds(g * (GT * D) + k * D, D)]).then_inc(s_dve, 1)
                    dve.wait_ge(s_dve, n.add(GT))
                    dve.sem_inc(s_apart, 1)
                    for k in range(GT):
                        dve.bn_aggr(mv[:, k, :], stats[:, k, :]).then_inc(s_var, 1)
                    dve.wait_ge(s_std, g + 1)
                    dve.reciprocal(rstd[:], std[:]).then_inc(s_dve, 1)
                    dve.wait_ge(s_dve, n.add())
                    for k in range(GT):
                        at = ds(g * (GT * D) + k * D, D)
                        dve.tensor_scalar(xh[:, at], res[:, at], mv[:, k, 0:1], rstd[:, k:k + 1],
                                          ALU.subtract, ALU.mult).then_inc(s_xn, 1)
                    dve.wait_ge(s_xn, g * GT + GT)
                    n.leave(NG)

                def heads(g):
                    at = ds(g * (GT * D), GT * D)
                    hv = xh[:, at].rearrange("p (h e) -> p h e", e=HD)
                    ndh = nd.rearrange("p (h e) -> p h e", e=HD)
                    wide = lambda a: a.unsqueeze(2).to_broadcast([P, GT * HEADS, HD])
                    dve.tensor_reduce(hsum, hv, AX, ALU.add).then_inc(s_dve, 1)
                    dve.wait_ge(s_dve, n.add())
                    dve.tensor_scalar(hsum, hsum, 1.0 / HD, None, ALU.mult).then_inc(s_dve, 1)
                    dve.wait_ge(s_dve, n.add())
                    if looped(g) or g >= 1:
                        dve.wait_ge(s_kvmm, g)
                    dve.tensor_tensor(ndh, hv, wide(hsum), ALU.subtract).then_inc(s_dev, 1)
                    rv = res[:, at].rearrange("p (t d) -> p t d", d=D)
                    dve.tensor_tensor(rv, rv, gb2_row.unsqueeze(1).to_broadcast([P, GT, D]), ALU.add).then_inc(s_dve, 1)
                    dve.wait_ge(s_dve, n.add())
                    dve.wait_ge(s_sq, g + 1)
                    dve.tensor_reduce(hsum, sq.rearrange("p (h e) -> p h e", e=HD), AX, ALU.add).then_inc(s_hss, 1)
                    dve.wait_ge(s_hstd, g + 1)
                    dve.tensor_scalar(hr, hstd, LN_EPS, None, ALU.add).then_inc(s_dve, 1)
                    dve.wait_ge(s_dve, n.add())
                    dve.reciprocal(hr, hr).then_inc(s_dve, 1)
                    dve.wait_ge(s_dve, n.add())
                    dve.tensor_tensor(ndh, ndh, wide(hr), ALU.mult).then_inc(s_nd, 1)
                    dve.wait_ge(s_nd, g + 1)

                at0 = n.n
                heads(0)
                per_group = n.n - at0
                with dve.Fori(1, NG) as g:
                    n.enter(g - 1, per_group)
                    heads(g)
                    n.leave(NG - 1)

                dve.wait_ge(s_kvmm, NG)
                for c in range(DC):
                    cols = slice(c * P, (c + 1) * P)
                    dve.tensor_copy(ncol[:, c:c + 1], bank[4 + c][:, 0:1]).then_inc(s_dve, 1)
                    dve.tensor_tensor(kvt[:, c, :], bank[2 + c][:, 0:P], vw_row[:, cols], ALU.mult).then_inc(s_dve, 1)
                    dve.tensor_tensor(kvs[:, c, :], bank[6][:, cols], vw_row[:, cols], ALU.mult).then_inc(s_dve, 1)
                    dve.wait_ge(s_dve, n.add(3))
                    dve.scalar_tensor_tensor(kvt[:, c, :], vb_row[:, cols], ncol[:, c:c + 1], kvt[:, c, :],
                                             ALU.mult, ALU.add).then_inc(s_dve, 1)
                    dve.scalar_tensor_tensor(kvs[:, c, :], vb_row[:, cols], float(N), kvs[:, c, :],
                                             ALU.mult, ALU.add).then_inc(s_dve, 1)
                    dve.wait_ge(s_dve, n.add(2))
                    dve.tensor_scalar(kvt[:, c, :], kvt[:, c, :], kw_col[:, c:c + 1], None, ALU.mult).then_inc(s_dve, 1)
                    dve.wait_ge(s_dve, n.add())
                    dve.scalar_tensor_tensor(kvt[:, c, :], kvs[:, c, :], kb_col[:, c:c + 1], kvt[:, c, :],
                                             ALU.mult, ALU.add).then_inc(s_dve, 1)
                    dve.wait_ge(s_dve, n.add())
                    dve.tensor_tensor(kvt[:, c, :], kvt[:, c, :], blockdiag, ALU.mult).then_inc(s_dve, 1)
                    dve.wait_ge(s_dve, n.add())
                    dve.tensor_tensor(kvm[:, c, :], kvt[:, c, :], ident[:], ALU.add).then_inc(s_dve, 1)
                    dve.wait_ge(s_dve, n.add())
                dve.tensor_scalar(lane_i[:], lane_i[:], 31, None, ALU.bitwise_and).then_inc(s_kv, 1)
                dve.wait_ge(s_kv, 1)
                dve.tensor_copy(lane32[:], lane_i[:]).then_inc(s_dve, 1)
                dve.wait_ge(s_dve, n.add())

                def residual(t, p):
                    dve.wait_ge(s_att, t + 1)
                    at = ds(t * D, D)
                    dve.tensor_tensor(res[:, at], res[:, at], bank[2 + p][:, 0:D], ALU.add).then_inc(s_res, 1)

                residual(0, 0)
                with dve.Fori(0, (NT - 1) // 2) as j:
                    residual(j * 2 + 1, 1)
                    residual(j * 2 + 2, 0)

        s_srec = sem("sorted_records_loaded")
        s_gw = sem("gin_weights_loaded")
        s_beta = sem("beta_loaded")
        s_gst = [sem(f"gather_staged{q}") for q in range(GBUF)]
        s_gath = [sem(f"edge_rows_landed{q}") for q in range(GBUF)]
        s_sel = sem("edge_matrix_built")
        s_sum = sem("edge_sums")
        s_acc = sem("edge_sums_added")
        SUMB = 8

        with nc.Block() as block:
            @block.sync
            def _(sp):
                sp.dma_start(sorted_rec.rearrange("p t c -> p (t c)"), rec_dram).then_inc(s_srec, 16)
                sp.dma_start(bucket_row, bucket_dram.rearrange("(o t) -> o t", o=1)).then_inc(s_bkld, 16)
                sp.dma_start(gW1_sb, gW1.rearrange("(c p) f -> p c f", p=P)).then_inc(s_gw, 16)
                sp.dma_start(gW2_sb, gW2.rearrange("(c p) d -> p c d", p=P)).then_inc(s_gw, 16)
                sp.dma_start(beta_row, row(beta)).then_inc(s_beta, 16)

            @block.scalar
            def _(act):
                def stage(r):
                    for q in range(GBUF):
                        if looped(r):
                            act.wait_ge(s_sum, r * ROUND + (q + 1 - GBUF) * GB)
                        act.activation(gath_idx[q], sorted_rec[:, ds(r * ROUND + q * GB, GB), 0],
                                       ACT.Copy).then_inc(s_gst[q], 1)

                act.wait_ge(s_srec, 16)
                stage(0)
                with act.Fori(1, EROUNDS) as r:
                    stage(r)

            @block.gpsimd
            def _(pool):
                with pool.Fori(0, EROUNDS) as r:
                    for q in range(GBUF):
                        pool.wait_ge(s_gst[q], r + 1)
                        pool.sem_inc(s_apart, 1)
                        for c in range(GB):
                            pool.indirect_dma_start(edge_rows[:, q * GB + c, :], None, xn_dram,
                                                    bass.IndirectOffsetOnAxis(gath_idx[q][:, c:c + 1], 0)
                                                    ).then_inc(s_gath[q], 16)

            @block.tensor
            def _(pe):
                def sums(r):
                    for c in range(ROUND):
                        if c % GB == 0:
                            pe.wait_ge(s_gath[c // GB], r * (16 * GB) + 16 * GB)
                        pe.wait_ge(s_sel, r * ROUND + c + 1)
                        if looped(r) or c >= SUMB:
                            pe.wait_ge(s_acc, r * ROUND + c + 1 - SUMB)
                        pe.matmul(bank[c % SUMB][:, 0:D], edge_sel[:, c, :], edge_rows[:, c, :],
                                  start=True, stop=True).then_inc(s_sum, 1)

                sums(0)
                with pe.Fori(1, EROUNDS) as r:
                    sums(r)

            @block.vector
            def _(dve):
                LEAD = ROUND // 2

                def build(r, c):
                    t = r * ROUND + c
                    dve.tensor_scalar(edge_sel[:, c % ROUND, :], iota_n[:], sorted_rec[:, ds(t, 1), 1],
                                      sorted_rec[:, ds(t, 1), 2], ALU.is_equal, ALU.mult).then_inc(s_sel, 1)

                def add(r, c, bucket):
                    t = r * ROUND + c
                    dve.wait_ge(s_sum, t + 1)
                    if looped(r) or r or c:
                        dve.wait_ge(s_acc, t)
                    at = ds(bucket * D, D)
                    dve.tensor_tensor(xh[:, at], xh[:, at], bank[c % SUMB][:, 0:D], ALU.add).then_inc(s_acc, 1)

                def rounds(r):
                    for q in range(GBUF):
                        _, buckets = nc.values_load_multi_w_load_instructions(
                            bucket_row[0:1, ds(r * ROUND + q * GB, GB)], engines=(nc.vector.engine,),
                            min_val=0, max_val=NT - 1,
                            skip_runtime_bounds_check_because="a count of buckets, limited to NT - 1")
                        for k in range(GB):
                            c = q * GB + k
                            if looped(r) or r * ROUND + c + LEAD < ET:
                                build(r, c + LEAD)
                            add(r, c, buckets[k])

                dve.wait_ge(s_srec, 16)
                for c in range(LEAD):
                    build(0, c)
                dve.wait_ge(s_bkld, 16)
                rounds(0)
                with dve.Fori(1, EROUNDS - 1) as r:
                    rounds(r)
                rounds(EROUNDS - 1)

        s_w1 = sem("w1_loaded")
        s_hin = sem("h_staged")
        s_hT = sem("h_transposed")
        s_hTe = sem("h_transpose_copied")
        s_g = sem("hidden_sums")
        s_gr = sem("hidden_rows")
        s_o = sem("mlp_rows")
        s_x2 = sem("x2_rows")
        s_x2b = sem("x2_plus_beta_rows")
        s_x2st = [sem(f"x2_stored{i}") for i in range(2)]
        s_var2 = sem("ln2_var")
        s_std2 = sem("ln2_std")
        s_xn2 = sem("xn2_rows")
        s_xn2k = sem("xn2_kept")
        s_x2T = sem("xn2_transposed")
        s_x2Te = sem("xn2_transpose_copied")
        s_l = sem("gate_sums")
        s_lg = sem("logits")
        s_w2 = sem("w2_loaded")
        s_xn2st = sem("xn2_stored")
        s_tri = sem("bf16_constants_made")
        s_hot = sem("choices")
        s_rank = sem("choice_ranks")
        s_place = sem("choice_ranks_read")
        s_slot = sem("choice_slots")
        s_ids = [sem(f"ids_staged{i}") for i in range(2)]
        s_idst = [sem(f"ids_landed{i}") for i in range(2)]

        def tile_at(j, k):
            return j * 2 + k, k % 2, j + k // 2

        def has(t):
            return looped(t) or 0 <= t < NT

        def over(v):
            return looped(v) or v > 0

        def run_steps(eng, step, first, last, j0, j1):
            for k in range(first, 2 * j0):
                step(0, k)
            with eng.Fori(j0, j1) as j:
                step(j, 0)
                step(j, 1)
            for k in range(2 * j1, last + 1):
                step(0, k)

        C_STEPS = (-2, NT + 4, 4, (NT - 3) // 2)
        W2G = 4
        W2_EARLY = (NT - 1) // W2G
        assert W2G * D == FC * D and NT - 1 == W2G * W2_EARLY
        w2_of = lambda e, n: w2[ds(e, n)].rearrange("e (m p) d -> p (e m) d", p=P)

        with nc.Block() as block:
            @block.sync
            def _(sp):
                sp.dma_start(w1_sb, w1.rearrange("e (c p) f -> p e c f", p=P)).then_inc(s_w1, 16)

                def store(t, p):
                    sp.wait_ge(s_x2b, t + 1)
                    sp.dma_start(x2b_dram[:, ds(t * D, D)], x2b[p]).then_inc(s_x2st[p], 16)

                def store_xn2(t):
                    sp.wait_ge(s_xn2k, t + 1)
                    sp.dma_start(xn2_dram[ds(t * P, P), :], xh[:, ds(t * D, D)]).then_inc(s_xn2st, 16)

                def group(g):
                    for k in range(W2G):
                        store(g * W2G + k, k % 2)
                        if looped(g) or g * W2G + k >= 2:
                            store_xn2(g * W2G + k - 2)
                    sp.wait_ge(s_x2, g * W2G + W2G)
                    sp.dma_start(upper[:, ds(g * (FC * D), FC * D)].rearrange("p (m d) -> p m d", d=D),
                                 w2_of(g, 1)).then_inc(s_w2, 16)

                group(0)
                with sp.Fori(1, W2_EARLY) as g:
                    group(g)
                store(NT - 1, (NT - 1) % 2)
                for t in range(NT - 3, NT):
                    store_xn2(t)
                for p in range(2):
                    sp.wait_ge(s_x2st[p], 16 * ((NT + 1 - p) // 2))
                sp.wait_ge(s_xn2st, 16 * NT)

            @block.gpsimd
            def _(pool):
                def step(j, k):
                    t, p, half = tile_at(j, k)
                    pool.wait_ge(s_slot, t + 1)
                    if over(half):
                        pool.wait_ge(s_idst[p], half * (16 * TOPK))
                    pool.sem_inc(s_apart, 1)
                    pool.tensor_copy(slot_idx[p][:], slot2[p][:]).then_inc(s_ids[p], 1)
                    pool.tensor_copy(slot_id[p][:], ids_all[:, ds(t * TOPK, TOPK)]).then_inc(s_ids[p], 1)
                    pool.wait_ge(s_ids[p], half * 2 + 2)
                    pool.sem_inc(s_apart, 1)
                    for c in range(TOPK):
                        pool.indirect_dma_start(ids_dram.rearrange("b (l o) -> (b l) o", o=1),
                                                bass.IndirectOffsetOnAxis(slot_idx[p][:, c:c + 1], 0),
                                                slot_id[p][:, c:c + 1], None).then_inc(s_idst[p], 16)

                run_steps(pool, step, 0, NT - 1, 1, (NT - 1) // 2)
                for p in range(2):
                    pool.wait_ge(s_idst[p], 16 * TOPK * ((NT + 1 - p) // 2))

            @block.tensor
            def _(pe):
                pe.wait_ge(s_gw, 32)
                pe.wait_ge(s_tri, 3)
                ranks = bank[1][:, 0:NX]

                def step(j, k):
                    t, p, _ = tile_at(j, k)
                    if has(t):
                        pe.wait_ge(s_hTe, t + 1)
                        if over(t - 1):
                            pe.wait_ge(s_gr, (t - 1) * HC)
                        for m in range(HC):
                            for c in range(DC):
                                mm = pe.matmul(bank[2 + p][:, m * P:(m + 1) * P], gW1_sb[:, c, m * P:(m + 1) * P],
                                               hT[p][:, c * P:(c + 1) * P], start=c == 0, stop=c == DC - 1)
                        mm.then_inc(s_g, 1)
                    t, p, _ = tile_at(j, k + 1)
                    if has(t):
                        pe.wait_ge(s_hin, t + 1)
                        if over(t - 1):
                            pe.wait_ge(s_hTe, t - 1)
                        for c in range(DC):
                            mm = pe.transpose(bank[0][:, p * D + c * P:p * D + (c + 1) * P], hin[p][:, c * P:(c + 1) * P], ident[:])
                        mm.then_inc(s_hT, 1)
                    t, p, _ = tile_at(j, k - 1)
                    if has(t):
                        pe.wait_ge(s_gr, t * HC + HC)
                        if over(t - 1):
                            pe.wait_ge(s_x2, t - 1)
                        for m in range(HC):
                            mm = pe.matmul(bank[4 + p][:, 0:D], g1[p][:, m * P:(m + 1) * P], gW2_sb[:, m, :],
                                           start=m == 0, stop=m == HC - 1)
                        mm.then_inc(s_o, 1)
                    t, p, _ = tile_at(j, k - 2)
                    if has(t):
                        pe.wait_ge(s_xn2, t + 1)
                        if over(t):
                            pe.wait_ge(s_x2Te, t)
                        for c in range(DC):
                            mm = pe.transpose(bank[6][:, c * P:(c + 1) * P], xn2[p][:, c * P:(c + 1) * P], ident[:])
                        mm.then_inc(s_x2T, 1)
                    t, p, _ = tile_at(j, k - 4)
                    if has(t):
                        pe.wait_ge(s_hot, t * 2 + 1)
                        if over(t):
                            pe.wait_ge(s_place, t)
                        pe.matmul(ranks, ones_pb, hot_sum[p], start=True, stop=False)
                        pe.matmul(ranks, before_b, hot_both[p], start=False, stop=True).then_inc(s_rank, 1)
                    t, p, _ = tile_at(j, k - 3)
                    if has(t):
                        pe.wait_ge(s_x2Te, t + 1)
                        if over(t):
                            pe.wait_ge(s_lg, t)
                        for c in range(DC):
                            mm = pe.matmul(bank[7][:, 0:NX], xn2T[p][:, c * P:(c + 1) * P], gate_sb[:, c, :],
                                           start=c == 0, stop=c == DC - 1)
                        mm.then_inc(s_l, 1)

                run_steps(pe, step, *C_STEPS)
                pe.wait_ge(s_hot, 2 * NT)
                pe.wait_ge(s_place, NT)
                pe.matmul(ranks, ones_pb, hot_sum[NT % 2], start=True, stop=True)

            @block.scalar
            def _(act):
                def step(j, k):
                    t, p, _ = tile_at(j, k)
                    if has(t):
                        act.wait_ge(s_g, t + 1)
                        if over(t - 1):
                            act.wait_ge(s_o, t - 1)
                        for m in range(HC):
                            act.activation(g1[p][:, m * P:(m + 1) * P], bank[2 + p][:, m * P:(m + 1) * P], ACT.Relu,
                                           bias=gb1_col[:, m:m + 1]).then_inc(s_gr, 1)
                    t, p, _ = tile_at(j, k + 1)
                    if has(t):
                        act.wait_ge(s_hT, t + 1)
                        if over(t - 1):
                            act.wait_ge(s_g, t - 1)
                        act.activation(hT[p], bank[0][:, p * D:(p + 1) * D], ACT.Copy).then_inc(s_hTe, 1)
                    t, p, _ = tile_at(j, k + 2)
                    if has(t):
                        if over(t - 1):
                            act.wait_ge(s_hT, t - 1)
                        act.activation(hin[p], xh[:, ds(t * D, D)], ACT.Copy).then_inc(s_hin, 1)
                    t, p, _ = tile_at(j, k - 1)
                    if has(t):
                        act.wait_ge(s_var2, t + 1)
                        act.activation(std2[p][:], mv2[p][:, 1:2], ACT.Sqrt, bias=eps_col[:]).then_inc(s_std2, 1)
                    t, p, _ = tile_at(j, k - 2)
                    if has(t):
                        act.wait_ge(s_x2T, t + 1)
                        if over(t - 1):
                            act.wait_ge(s_l, t - 1)
                        act.activation(xn2T[p], bank[6][:, 0:D], ACT.Copy).then_inc(s_x2Te, 1)
                        act.activation(xh[:, ds(t * D, D)], xn2[p], ACT.Copy).then_inc(s_xn2k, 1)

                run_steps(act, step, *C_STEPS)

            @block.vector
            def _(dve):
                n = dve_n
                dve.tensor_copy(before_b, before[:]).then_inc(s_tri, 1)
                dve.memset(ones_pb, 1.0).then_inc(s_tri, 1)
                dve.memset(hot_sum[0], 0.0).then_inc(s_tri, 1)
                dve.wait_ge(s_tri, 3)
                dve.wait_ge(s_beta, 16)

                def step(j, k):
                    t, p, half = tile_at(j, k - 1)
                    t3, p3, half3 = tile_at(j, k - 3)
                    t5, p5, half5 = tile_at(j, k - 5)
                    if has(t5):
                        dve.wait_ge(s_rank, t5 + 1)
                        dve.tensor_tensor(place, bank[1][:, 0:NX], expert_at[:], ALU.add).then_inc(s_place, 1)
                    if has(t):
                        dve.wait_ge(s_o, t + 1)
                        if over(t - 1):
                            dve.wait_ge(s_xn2k, t - 1)
                        dve.tensor_tensor(x2[p], res[:, ds(t * D, D)], bank[4 + p][:, 0:D], ALU.add).then_inc(s_x2, 1)
                    if has(t3):
                        dve.wait_ge(s_l, t3 + 1)
                        dve.tensor_tensor(logits[:], bank[7][:, 0:NX], gateb_row[:], ALU.add).then_inc(s_lg, 1)
                    if has(t):
                        dve.wait_ge(s_x2, t + 1)
                        dve.bn_stats(st2[:], x2[p]).then_inc(s_dve, 1)
                        stats_at = n.add()
                    if has(t3):
                        dve.wait_ge(s_lg, t3 + 1)
                        dve.sem_inc(s_apart, 1)
                        dve.max(top8[:], logits[:]).then_inc(s_dve, 1)
                        max_at = n.add()
                    if has(t5):
                        dve.wait_ge(s_place, t5 + 1)
                        if over(t5):
                            dve.wait_ge(s_slot, t5)
                        dve.tensor_tensor(hot_place, hot[p5], place.unsqueeze(1).to_broadcast([P, TOPK, NX]),
                                          ALU.mult).then_inc(s_dve, 1)
                        hot_at = n.add()
                    if has(t):
                        dve.wait_ge(s_dve, stats_at)
                        dve.sem_inc(s_apart, 1)
                        dve.bn_aggr(mv2[p][:], st2[:]).then_inc(s_var2, 1)
                    if has(t3):
                        dve.wait_ge(s_dve, max_at)
                        dve.sem_inc(s_apart, 1)
                        dve.max_index(idx8[:], top8[:], logits[:]).then_inc(s_dve, 1)
                        dve.tensor_copy(topv[:, ds(t3 * TOPK, TOPK)], top8[:, 0:TOPK]).then_inc(s_dve, 1)
                        index_at = n.add()
                        n.add()
                    if has(t5):
                        if over(half5):
                            dve.wait_ge(s_ids[p5], half5 * 2)
                        dve.wait_ge(s_dve, hot_at)
                        dve.tensor_reduce(slot2[p5][:], hot_place, AX, ALU.add).then_inc(s_slot, 1)
                    if has(t3):
                        dve.wait_ge(s_dve, index_at)
                        dve.tensor_copy(top_f[p3][:], idx8[:, 0:TOPK]).then_inc(s_dve, 1)
                        top_at = n.add()
                    if has(t):
                        if over(half):
                            dve.wait_ge(s_x2st[p], half * 16)
                        dve.tensor_tensor(x2b[p], x2[p], beta_row, ALU.add).then_inc(s_x2b, 1)
                    if has(t3):
                        dve.wait_ge(s_dve, top_at)
                        dve.tensor_tensor(hot[p3], top_f[p3][:].unsqueeze(2).to_broadcast([P, TOPK, NX]),
                                          iota_n[:, 0:NX].unsqueeze(1).to_broadcast([P, TOPK, NX]),
                                          ALU.is_equal).then_inc(s_dve, 1)
                        hot3_at = n.add()
                    if has(t):
                        dve.wait_ge(s_std2, t + 1)
                        dve.reciprocal(rstd2[:], std2[p][:]).then_inc(s_dve, 1)
                        rstd_at = n.add()
                    if has(t3):
                        dve.wait_ge(s_dve, hot3_at)
                        dve.tensor_tensor(hot_both[p3], hot[p3][:, 0, :], hot[p3][:, 1, :], ALU.add).then_inc(s_hot, 1)
                        hot_both_at = t3 * 2 + 1
                    if has(t):
                        dve.wait_ge(s_dve, rstd_at)
                        dve.tensor_scalar(xn2[p], x2[p], mv2[p][:, 0:1], rstd2[:], ALU.subtract, ALU.mult).then_inc(s_xn2, 1)
                        dve.wait_ge(s_xn2, t + 1)
                    if has(t3):
                        dve.wait_ge(s_hot, hot_both_at)
                        if over(t3):
                            dve.wait_ge(s_rank, t3)
                        dve.tensor_tensor(hot_sum[1 - p3], hot_sum[p3], hot_both[p3], ALU.add).then_inc(s_hot, 1)

                first, last, j0, j1 = C_STEPS
                for k in range(first, 2 * j0):
                    step(0, k)
                with dve.Fori(j0, j1) as j:
                    n.enter(j - j0, 2 * 8)
                    step(j, 0)
                    step(j, 1)
                    n.leave(j1 - j0)
                for k in range(2 * j1, last + 1):
                    step(0, k)

        s_gap = sem("gate_gaps")
        s_gape = sem("gate_exps")
        s_block = sem("id_blocks")
        s_idt = sem("tile_ids_loaded")
        s_wide = sem("tile_experts")
        s_row = sem("tile_expert_rows")
        s_pick = sem("bias_picks")
        s_b1 = sem("first_biases")
        s_turn = sem("tile_ids_transposed")
        s_tiles = sem("tile_tables")
        W2_LATE = NX - W2_EARLY

        with nc.Block() as block:
            @block.sync
            def _(sp):
                sp.dma_start(upper[:, W2_EARLY * (FC * D):NX * (FC * D)].rearrange("p (m d) -> p m d", d=D),
                             w2_of(W2_EARLY, W2_LATE)).then_inc(s_w2, 16)

            @block.gpsimd
            def _(pool):
                pool.wait_ge(s_block, 1)
                pool.indirect_dma_start(ids_tile[0:XT, :], None, ids_dram,
                                        bass.IndirectOffsetOnAxis(block_i[0:XT, :], 0)).then_inc(s_idt, 16)

            @block.tensor
            def _(pe):
                pe.wait_ge(s_wide, 1)
                pe.matmul(bank[0][0:96, 0:P], expert_wide, ident[:], start=True, stop=True).then_inc(s_row, 1)
                pe.wait_ge(s_pick, 2)
                for m in range(FC):
                    mm = pe.matmul(bank[2][:, m * XT:(m + 1) * XT], bias_split[:, m * P:(m + 1) * P], pick_all[:, 0:XT],
                                   start=True, stop=True)
                mm.then_inc(s_b1, 1)
                pe.wait_ge(s_idt, 16)
                pe.transpose(bank[3][:, 0:XT], ids_tile[0:XT, :], ident[0:XT, 0:XT]).then_inc(s_turn, 1)

            @block.scalar
            def _(act):
                act.wait_ge(s_gap, 1)
                act.activation(gap_e, gap, ACT.Exp).then_inc(s_gape, 1)

            @block.vector
            def _(dve):
                n = dve_n
                tv = topv[:].rearrange("p (t k) -> p t k", k=TOPK)
                mw = mix_w[:].rearrange("p (t k) -> p t k", k=TOPK)
                tile_ends(dve, NX, bank[1][:, 0:NX])
                dve.tensor_tensor(past_x, iota_pc[:, 0:1].to_broadcast([P, NX - 1]), ends[:, 0:NX - 1],
                                  ALU.is_ge).then_inc(s_dve, 1)
                dve.wait_ge(s_dve, n.add())
                dve.tensor_reduce(tile_expert[:], past_x, AX, ALU.add).then_inc(s_dve, 1)
                dve.tensor_tensor(past_tiles, past_x, tiles_f[:, 0:NX - 1], ALU.mult).then_inc(s_dve, 1)
                dve.wait_ge(s_dve, n.add(2))
                dve.tensor_copy(expert_wide, tile_expert[:].to_broadcast([P, 96])).then_inc(s_wide, 1)
                dve.tensor_reduce(first_tile, past_tiles, AX, ALU.add).then_inc(s_dve, 1)
                dve.tensor_scalar(block_f, tile_expert[:], float(NT), iota_pc[:, 0:1], ALU.mult, ALU.add).then_inc(s_dve, 1)
                dve.wait_ge(s_dve, n.add(2))
                dve.tensor_tensor(block_f, block_f, first_tile, ALU.subtract).then_inc(s_dve, 1)
                dve.wait_ge(s_dve, n.add())
                dve.tensor_copy(block_i, block_f).then_inc(s_block, 1)
                dve.wait_ge(s_row, 1)
                dve.tensor_copy(expert_row[:], bank[0][0:1, 0:P]).then_inc(s_pick, 1)
                dve.tensor_scalar(pick_all[:], bank[0][0:96, 0:P], lane32[:], None, ALU.is_equal).then_inc(s_pick, 1)
                dve.tensor_tensor(gap, tv[:, :, 1], tv[:, :, 0], ALU.subtract).then_inc(s_gap, 1)
                dve.wait_ge(s_gape, 1)
                dve.tensor_scalar(gap_s, gap_e, 1.0, None, ALU.add).then_inc(s_dve, 1)
                dve.wait_ge(s_dve, n.add())
                dve.reciprocal(gap_s, gap_s).then_inc(s_dve, 1)
                dve.wait_ge(s_dve, n.add())
                dve.tensor_copy(mw[:, :, 0], gap_s).then_inc(s_dve, 1)
                dve.tensor_tensor(mw[:, :, 1], gap_e, gap_s, ALU.mult).then_inc(s_dve, 1)
                dve.wait_ge(s_b1, 1)
                dve.tensor_copy(b1_tile[:], bank[2][:, 0:FC * XT]).then_inc(s_dve, 1)
                ids = bank[3][:, 0:XT]
                dve.wait_ge(s_turn, 1)
                dve.tensor_scalar(second, ids, float(NTP), -float(NTP), ALU.is_ge, ALU.mult).then_inc(s_dve, 1)
                dve.tensor_scalar(pad, ids, float(TOPK * NTP), None, ALU.is_ge).then_inc(s_dve, 1)
                dve.wait_ge(s_dve, n.add(5))
                dve.tensor_tensor(node1, ids, second, ALU.add).then_inc(s_dve, 1)
                dve.tensor_tensor(pad_tile, pad, iota_n[:, 0:XT], ALU.mult).then_inc(s_dve, 1)
                dve.wait_ge(s_dve, n.add(2))
                dve.scalar_tensor_tensor(node_all[:], pad, -float(NTP), node1, ALU.mult, ALU.add).then_inc(s_tiles, 1)
                dve.scalar_tensor_tensor(dest_all[:], pad_tile, float(P), ids, ALU.mult, ALU.add).then_inc(s_tiles, 1)
                dve.wait_ge(s_tiles, 2)

        s_tki = [sem(f"row_index_staged{i}") for i in range(2)]
        s_tok = [sem(f"rows_landed{i}") for i in range(2)]
        s_tT = sem("rows_transposed")
        s_tTe = sem("rows_transpose_copied")
        s_w1t = sem("tile_w1_copied")
        s_pk = sem("bias_pick")
        s_h = sem("expert_hidden_sums")
        s_hr = sem("expert_hidden")
        s_y = sem("expert_sums")
        s_yr = sem("expert_rows")
        s_ydi = [sem(f"result_index_staged{i}") for i in range(2)]
        s_yst = [sem(f"expert_rows_scattered{i}") for i in range(2)]
        assert XT % 2 == 0
        E_STEPS = (-2, XT, 2, (XT - 2) // 2)
        AHEAD = 4
        G_STEPS = (-AHEAD, XT, 2, (XT - AHEAD) // 2)

        def is_tile(t):
            return looped(t) or 0 <= t < XT

        with nc.Block() as block:
            @block.gpsimd
            def _(pool):
                def step(j, k):
                    t, p, half = tile_at(j, k - 1)
                    if is_tile(t):
                        if over(half):
                            pool.wait_ge(s_yst[p], half * 16)
                        pool.sem_inc(s_apart, 1)
                        pool.tensor_copy(dest_idx[p][:], dest_all[:, ds(t, 1)]).then_inc(s_ydi[p], 1)
                    t, p, half = tile_at(j, k + AHEAD)
                    if is_tile(t):
                        if over(half):
                            pool.wait_ge(s_tok[p], half * 16)
                        pool.sem_inc(s_apart, 1)
                        pool.tensor_copy(tok_idx[p][:], node_all[:, ds(t, 1)]).then_inc(s_tki[p], 1)
                    t, p, half = tile_at(j, k - 1)
                    if is_tile(t):
                        pool.wait_ge(s_ydi[p], half + 1)
                        pool.wait_ge(s_yr, t + 1)
                        pool.sem_inc(s_apart, 1)
                        pool.indirect_dma_start(y_dram, bass.IndirectOffsetOnAxis(dest_idx[p][:], 0),
                                                yrow[p], None).then_inc(s_yst[p], 16)
                    t, p, half = tile_at(j, k + AHEAD)
                    if is_tile(t):
                        pool.wait_ge(s_tki[p], half + 1)
                        if over(t - 1):
                            pool.wait_ge(s_tT, t - 1)
                        pool.sem_inc(s_apart, 1)
                        pool.indirect_dma_start(tok[p], None, xn2_dram,
                                                bass.IndirectOffsetOnAxis(tok_idx[p][:], 0)).then_inc(s_tok[p], 16)

                run_steps(pool, step, *G_STEPS)
                for p in range(2):
                    pool.wait_ge(s_yst[p], 16 * (XT // 2))

            @block.tensor
            def _(pe):
                pe.wait_ge(s_w2, 16 * (W2_EARLY + 1))
                pe.wait_ge(s_pick, 2)

                def step(j, k):
                    t, p, _ = tile_at(j, k)
                    if is_tile(t):
                        pe.wait_ge(s_tTe, t + 1)
                        pe.wait_ge(s_w1t, t + 1)
                        if over(t - 1):
                            pe.wait_ge(s_hr, (t - 1) * FC)
                        for m in range(FC):
                            for c in range(DC):
                                mm = pe.matmul(bank[2 + p][:, m * P:(m + 1) * P],
                                               w1_tile[p][:, c * F + m * P:c * F + (m + 1) * P],
                                               tokT[p][:, c * P:(c + 1) * P], start=c == 0, stop=c == DC - 1)
                        mm.then_inc(s_h, 1)
                    t, p, half = tile_at(j, k + 2)
                    if is_tile(t):
                        pe.wait_ge(s_tok[p], half * 16 + 16)
                        if over(t - 1):
                            pe.wait_ge(s_tTe, t - 1)
                        for c in range(DC):
                            mm = pe.transpose(bank[p][:, c * P:(c + 1) * P], tok[p][:, c * P:(c + 1) * P], ident[:])
                        mm.then_inc(s_tT, 1)
                    t, p, _ = tile_at(j, k - 1)
                    if is_tile(t):
                        e = pe.value_load(expert_row[0:1, ds(t, 1)], min_val=0, max_val=NX - 1)
                        pe.wait_ge(s_pk, t + 1)
                        if over(t - 1):
                            pe.wait_ge(s_yr, t - 1)
                        pe.matmul(bank[6 + p][:, 0:D], pick[p], bias_split[:, F:F + D], start=True, stop=False)
                        pe.wait_ge(s_hr, t * FC + FC)
                        for m in range(FC):
                            mm = pe.matmul(bank[6 + p][:, 0:D], hidT[p][:, m * P:(m + 1) * P],
                                           upper[:, ds(e * (FC * D) + m * D, D)], start=False, stop=m == FC - 1)
                        mm.then_inc(s_y, 1)

                run_steps(pe, step, *E_STEPS)

            @block.scalar
            def _(act):
                act.wait_ge(s_w1, 16)
                act.wait_ge(s_pick, 2)

                def step(j, k):
                    t, p, _ = tile_at(j, k + 1)
                    if is_tile(t):
                        e = act.value_load(expert_row[0:1, ds(t, 1)], min_val=0, max_val=NX - 1)
                        if over(t - 1):
                            act.wait_ge(s_h, t - 1)
                        act.activation(w1_tile[p], lower[:, ds(e * (DC * F), DC * F)], ACT.Copy).then_inc(s_w1t, 1)
                    t, p, _ = tile_at(j, k + 2)
                    if is_tile(t):
                        act.wait_ge(s_tT, t + 1)
                        if over(t - 1):
                            act.wait_ge(s_h, t - 1)
                        act.activation(tokT[p], bank[p][:, 0:D], ACT.Copy).then_inc(s_tTe, 1)

                run_steps(act, step, *E_STEPS)

            @block.vector
            def _(dve):
                def step(j, k):
                    t, p, _ = tile_at(j, k)
                    if is_tile(t):
                        dve.wait_ge(s_h, t + 1)
                        if over(t - 1):
                            dve.wait_ge(s_y, t - 1)
                        for m in range(FC):
                            dve.tensor_scalar(hidT[p][:, m * P:(m + 1) * P], bank[2 + p][:, m * P:(m + 1) * P],
                                              b1_tile[:, ds(t + m * XT, 1)], 0.0, ALU.add, ALU.max).then_inc(s_hr, 1)
                        dve.tensor_scalar(pick[p], ones_b[:], pick_all[:, ds(t, 1)], None, ALU.mult).then_inc(s_pk, 1)
                    t, p, half = tile_at(j, k - 1)
                    if is_tile(t):
                        dve.wait_ge(s_y, t + 1)
                        if over(half):
                            dve.wait_ge(s_yst[p], half * 16)
                        dve.tensor_copy(yrow[p], bank[6 + p][:, 0:D]).then_inc(s_yr, 1)

                run_steps(dve, step, *E_STEPS)

        s_gamma = sem("gamma_loaded")
        s_frow = [sem(f"expert_rows_loaded{h}") for h in range(2)]
        s_fx2 = [sem(f"x2_loaded{h}") for h in range(2)]
        s_fmix = [sem(f"rows_mixed{h}") for h in range(2)]
        s_fvar = [sem(f"ln3_var{h}") for h in range(2)]
        s_fstd = [sem(f"ln3_std{h}") for h in range(2)]
        s_fnorm = [sem(f"rows_normed{h}") for h in range(2)]
        s_fscale = [sem(f"rows_scaled{h}") for h in range(2)]
        s_fout = [sem(f"rows_out{h}") for h in range(2)]
        s_fost = [sem(f"rows_out_stored{h}") for h in range(2)]

        with nc.Block() as block:
            @block.scalar
            def _(act):
                def rounds(r):
                    for h, (k0, m) in enumerate(HALVES):
                        act.wait_ge(s_fvar[h], r * m + m)
                        act.activation(std[:, k0:k0 + m], mv[:, k0:k0 + m, 1], ACT.Sqrt, bias=eps_col[:]).then_inc(s_fstd[h], 1)

                with act.Fori(0, NG) as r:
                    rounds(r)

            @block.sync
            def _(sp):
                def load(r, h):
                    k0, m = HALVES[h]
                    if looped(r) or r >= 1:
                        sp.wait_ge(s_fmix[h], r * m)
                    for k in range(TOPK):
                        sp.dma_start(exp_rows[:, k, k0:k0 + m, :],
                                     y_dram[ds(r * (GT * P) + (k * NTP + k0 * P), m * P), :]
                                     .rearrange("(t p) d -> p t d", p=P)).then_inc(s_frow[h], 16)
                    if looped(r) or r >= 1:
                        sp.wait_ge(s_fout[h], r)
                    sp.dma_start(x2b_in[:, k0:k0 + m, :].rearrange("p s d -> p (s d)"),
                                 x2b_dram[:, ds(r * (GT * D) + k0 * D, m * D)]).then_inc(s_fx2[h], 16)

                def store(r, h):
                    k0, m = HALVES[h]
                    sp.wait_ge(s_fout[h], r + 1)
                    whole = m if looped(r) or r * GT + k0 + m < NT else m - 1
                    sp.dma_start(out[ds(r * (GT * P) + k0 * P, whole * P), :].rearrange("(t p) d -> p t d", p=P),
                                 out_rows[:, k0:k0 + whole, :]).then_inc(s_fost[h], 16)
                    if whole < m:
                        sp.dma_start(out[(NT - 1) * P:N, :], out_rows[0:TAIL, k0 + whole, :]).then_inc(s_fost[h], 16)

                load(0, 0)
                sp.dma_start(gamma_row, row(gamma)).then_inc(s_gamma, 16)
                load(0, 1)
                with sp.Fori(1, NG) as r:
                    for h in range(2):
                        load(r, h)
                        store(r - 1, h)
                store(NG - 1, 0)
                store(NG - 1, 1)
                sp.wait_ge(s_fost[0], 16 * NG)
                sp.wait_ge(s_fost[1], 16 * (NG + 1))

            @block.vector
            def _(dve):
                n = dve_n

                def half(r, h):
                    k0, m = HALVES[h]
                    dve.wait_ge(s_frow[h], r * (16 * TOPK) + 16 * TOPK)
                    for k in range(m):
                        dve.scalar_tensor_tensor(mixed[:, k0 + k, :], exp_rows[:, 0, k0 + k, :],
                                                 mix_w[:, ds(r * (GT * TOPK) + (k0 + k) * TOPK, 1)],
                                                 xh[:, ds(r * (GT * D) + (k0 + k) * D, D)], ALU.mult, ALU.add).then_inc(s_dve, 1)
                    n.add(m)
                    for k in range(m):
                        dve.wait_ge(s_dve, n.back(m - 1 - k))
                        dve.scalar_tensor_tensor(mixed[:, k0 + k, :], exp_rows[:, 1, k0 + k, :],
                                                 mix_w[:, ds(r * (GT * TOPK) + (k0 + k) * TOPK + 1, 1)],
                                                 mixed[:, k0 + k, :], ALU.mult, ALU.add).then_inc(s_fmix[h], 1)
                    for k in range(m):
                        dve.wait_ge(s_fmix[h], r * m + k + 1)
                        dve.bn_stats(stats[:, k0 + k, :], mixed[:, k0 + k, :]).then_inc(s_dve, 1)
                    n.add(m)
                    for k in range(m):
                        dve.wait_ge(s_dve, n.back(m - 1 - k))
                        dve.sem_inc(s_apart, 1)
                        dve.bn_aggr(mv[:, k0 + k, :], stats[:, k0 + k, :]).then_inc(s_fvar[h], 1)

                def finish(r, h):
                    k0, m = HALVES[h]
                    dve.wait_ge(s_fstd[h], r + 1)
                    dve.reciprocal(rstd[:, k0:k0 + m], std[:, k0:k0 + m]).then_inc(s_dve, 1)
                    dve.wait_ge(s_dve, n.add())
                    for k in range(k0, k0 + m):
                        dve.tensor_scalar(normed[:, k, :], mixed[:, k, :], mv[:, k, 0:1], rstd[:, k:k + 1],
                                          ALU.subtract, ALU.mult).then_inc(s_dve, 1)
                    dve.wait_ge(s_dve, n.add(m))
                    nv, ov = normed[:, k0:k0 + m, :], out_rows[:, k0:k0 + m, :]
                    dve.tensor_tensor(nv, nv, gamma_row.unsqueeze(1).to_broadcast([P, m, D]), ALU.mult).then_inc(s_dve, 1)
                    dve.wait_ge(s_dve, n.add())
                    dve.wait_ge(s_fx2[h], r * 16 + 16)
                    if looped(r) or r >= 1:
                        dve.wait_ge(s_fost[h], r * 16)
                    dve.tensor_tensor(ov, nv, x2b_in[:, k0:k0 + m, :], ALU.add).then_inc(s_fout[h], 1)
                    dve.wait_ge(s_fout[h], r + 1)

                def rounds(r):
                    half(r, 0)
                    half(r, 1)
                    finish(r, 0)
                    finish(r, 1)

                dve.wait_ge(s_gamma, 16)
                at0 = n.n
                rounds(0)
                per_round = n.n - at0
                with dve.Fori(1, NG) as r:
                    n.enter(r - 1, per_round)
                    rounds(r)
                    n.leave(NG - 1)


_INS = ["x", "src", "dst", "edge_weight", "L0_gnn_W1", "L0_gnn_b1", "L0_gnn_W2", "L0_gnn_b2",
        "L0_mix_kln_weight", "L0_mix_kln_bias", "L0_mix_vln_weight", "L0_mix_vln_bias",
        "L0_ffn_gate_w", "L0_ffn_gate_b", "L0_ffn_w1", "L0_ffn_b1", "L0_ffn_w2", "L0_ffn_b2",
        "L0_ffn_gamma", "L0_ffn_beta"]


def kernel(**inputs):
    import numpy as _np
    import concourse.bacc as _bacc
    from concourse import mybir as _mybir
    from concourse.bass_utils import run_bass_kernel_spmd as _run

    nc = _bacc.Bacc("TRN2", target_bir_lowering=False, num_devices=1)
    arrays, args = {}, []
    for name in _INS:
        a = _np.ascontiguousarray(inputs[name])
        arrays[f"in_{name}"] = a
        args.append(nc.dram_tensor(f"in_{name}", a.shape, _mybir.dt.from_np(a.dtype), kind="ExternalInput").ap())
    out = nc.dram_tensor("out_rows_dram", inputs["x"].shape, _mybir.dt.float32, kind="ExternalOutput").ap()
    gps_layer(nc, *args, out)
    r = _run(nc, [arrays], core_ids=[0])
    return r.results[0]["out_rows_dram"]
```
